# Optimizing a Trainium2 kernel written in Bass

```python
import numpy as np
import jax
import jax.numpy as jnp

def _softmax(x, axis=-1):
    return jax.nn.softmax(x, axis=axis)

def _gelu(x):
    return jax.nn.gelu(x, approximate=True)

def _silu(x):
    return jax.nn.silu(x)

def _sigmoid(x):
    return jax.nn.sigmoid(x)

def _layernorm(x, axis=-1, eps=1e-05):
    m = jnp.mean(x, axis=axis, keepdims=True)
    v = jnp.var(x, axis=axis, keepdims=True)
    return (x - m) / jnp.sqrt(v + eps)

def _scatter_add(tgt, idx, src, axis=0):
    return tgt.at[idx].add(src)

def _segment_sum(src, seg, n):
    return jax.ops.segment_sum(src, seg, n)
kernel_name = 'mk_decoder_postln_d1_seqx_r8_4ce92a'

def setup_inputs(seed: int=0):
    np.random.seed(seed)
    _w = jnp.asarray

    def _rec_inputs():
        import jax
        import jax.numpy as jnp
        _rk = jax.random.key(seed)
        x = 7.22e-05 + 1 * jax.random.normal(jax.random.fold_in(_rk, 1), (16, 64, 256), jnp.float32)
        _lenS = 64 - jax.random.randint(jax.random.fold_in(_rk, 7), (16,), 0, max(1, 64 // 4) + 1, jnp.int32)
        _lenS2 = 64 - jax.random.randint(jax.random.fold_in(_rk, 8), (16,), 0, max(1, 64 // 4) + 1, jnp.int32)
        _ctx_512P = jax.random.normal(jax.random.fold_in(_rk, 11), (16, 16, 64), jnp.float32)
        _ctx_512c = jax.random.dirichlet(jax.random.fold_in(_rk, 511), 0.3 * jnp.ones((16,), jnp.float32), (16, 64))
        _ctx_512t = jnp.einsum('bsk,bkd->bsd', _ctx_512c, _ctx_512P)
        _ctx_512t = _ctx_512t * jax.lax.rsqrt(jnp.mean(jnp.square(_ctx_512t)) + 1e-12) * 0.953939
        ctx_512 = -0.000514642 + 1.00011 * (_ctx_512t + 0.3 * jax.random.normal(jax.random.fold_in(_rk, 611), (16, 64, 64), jnp.float32))
        return (x, ctx_512)
    x, ctx_512 = _rec_inputs()

    def _L0_attn_setup():
        import jax, jax.numpy as jnp
        import numpy as np
        B, N, HID, H, D = (2, 1024, 256, 16, 128)
        BLOCK = 32
        EPS = 1e-06

        def _alibi_slopes(h):
            start = 2.0 ** (-2.0 ** (-(np.log2(h) - 3)))
            return np.array([start * start ** i for i in range(h)], dtype=np.float32)

        def _lightning_attention(q, k, v, slope_rate):
            b, h, n, d = q.shape
            nb = n // BLOCK
            s = slope_rate.reshape(1, h, 1, 1).astype(q.dtype)
            arr = jnp.arange(1, BLOCK + 1, dtype=q.dtype)
            q_decay = jnp.exp(-s * arr[None, None, :, None])
            k_decay = jnp.exp(-s * (BLOCK - arr)[None, None, :, None])
            idx = arr[:, None] - arr[None, :]
            diag_decay = jnp.where(idx[None, None] >= 0, jnp.exp(-s * idx[None, None]), 0.0)
            block_decay = jnp.exp(-s * BLOCK)

            def to_blocks(x):
                return x.reshape(b, h, nb, BLOCK, d).transpose(2, 0, 1, 3, 4)
            qb, kb, vb = (to_blocks(q), to_blocks(k), to_blocks(v))

            def step(kv, blk):
                qi, ki, vi = blk
                inter = jnp.einsum('bhld,bhde->bhle', qi * q_decay, kv)
                qk = jnp.einsum('bhld,bhmd->bhlm', qi, ki) * diag_decay
                intra = jnp.einsum('bhlm,bhme->bhle', qk, vi)
                kv = block_decay * kv + jnp.einsum('bhld,bhle->bhde', ki * k_decay, vi)
                return (kv, inter + intra)
            kv0 = jnp.zeros((b, h, d, d), q.dtype)
            _, out = jax.lax.scan(step, kv0, (qb, kb, vb))
            return out.transpose(1, 2, 0, 3, 4).reshape(b, h, n, d)
        key = jax.random.key(seed)
        k1, k2, k3, k4 = jax.random.split(key, 4)
        scale = 0.02
        hidden_states = jax.random.normal(k1, (B, N, HID), jnp.float32)
        w_qkv = jax.random.normal(k2, (HID, 3 * H * D), jnp.float32) * scale
        w_gate = jax.random.normal(k3, (HID, H * D), jnp.float32) * scale
        w_out = jax.random.normal(k4, (H * D, HID), jnp.float32) * scale
        rms_weight = jnp.ones((H * D,), jnp.float32)
        slope_rate = jnp.asarray(_alibi_slopes(H)).reshape(H, 1, 1) * (1.0 + 1e-05)
        return dict(hidden_states=hidden_states, slope_rate=slope_rate, w_qkv=w_qkv, w_gate=w_gate, w_out=w_out, rms_weight=rms_weight)
    _L0_attn_all = _L0_attn_setup()
    _L0_attn_in = {k: v for k, v in _L0_attn_all.items() if k in ('slope_rate', 'w_qkv', 'w_gate', 'w_out', 'rms_weight')}
    del _L0_attn_all

    def _L0_xattn_setup():
        import jax, jax.numpy as jnp
        import numpy as np
        import math
        D_MODEL = 256
        N_HEADS = 16
        N_GROUPS = 4
        HEADS_PER_GROUP = N_HEADS // N_GROUPS
        HEAD_DIM = D_MODEL // N_HEADS
        B, S = (2, 256)
        key = jax.random.key(seed)
        k1, k2, k3, k4, k5 = jax.random.split(key, 5)
        q = jax.random.normal(k1, (B, S, D_MODEL), dtype=jnp.float32)
        k = jax.random.normal(k2, (B, S, N_GROUPS * HEAD_DIM), dtype=jnp.float32)
        v = jax.random.normal(k3, (B, S, N_GROUPS * HEAD_DIM), dtype=jnp.float32)
        lim = 1.0 / math.sqrt(D_MODEL)
        Wc = jax.random.uniform(k4, (D_MODEL, D_MODEL), minval=-lim, maxval=lim, dtype=jnp.float32)
        bc = jax.random.uniform(k5, (D_MODEL,), minval=-lim, maxval=lim, dtype=jnp.float32)
        return {'q': q, 'k': k, 'v': v, 'Wc': Wc, 'bc': bc}
    _L0_xattn_all = _L0_xattn_setup()
    _L0_xattn_in = {k: v for k, v in _L0_xattn_all.items() if k in ('Wc', 'bc')}
    del _L0_xattn_all

    def _L0_ffn_setup():
        import jax, jax.numpy as jnp
        import numpy as np
        NUM_EXPERTS = 8
        TOP_K = 2
        HIDDEN = 256
        INTER = 704
        B, S = (4, 256)
        key = jax.random.key(seed)
        ks = jax.random.split(key, 5)
        scale_h = 1.0 / np.sqrt(HIDDEN)
        scale_i = 1.0 / np.sqrt(INTER)
        return {'hidden_states': jax.random.normal(ks[0], (B, S, HIDDEN), dtype=jnp.float32), 'Wg': jax.random.normal(ks[1], (NUM_EXPERTS, HIDDEN), dtype=jnp.float32) * scale_h, 'w1': jax.random.normal(ks[2], (NUM_EXPERTS, INTER, HIDDEN), dtype=jnp.float32) * scale_h, 'w3': jax.random.normal(ks[3], (NUM_EXPERTS, INTER, HIDDEN), dtype=jnp.float32) * scale_h, 'w2': jax.random.normal(ks[4], (NUM_EXPERTS, HIDDEN, INTER), dtype=jnp.float32) * scale_i}
    _L0_ffn_all = _L0_ffn_setup()
    _L0_ffn_in = {k: v for k, v in _L0_ffn_all.items() if k in ('Wg', 'w1', 'w3', 'w2')}
    del _L0_ffn_all
    return {'x': x, 'ctx_512': ctx_512, 'L0_attn_slope_rate': _L0_attn_in['slope_rate'], 'L0_attn_w_qkv': _L0_attn_in['w_qkv'], 'L0_attn_w_gate': _L0_attn_in['w_gate'], 'L0_attn_w_out': _L0_attn_in['w_out'], 'L0_attn_rms_weight': _L0_attn_in['rms_weight'], 'L0_xattn_Wc': _L0_xattn_in['Wc'], 'L0_xattn_bc': _L0_xattn_in['bc'], 'L0_ffn_Wg': _L0_ffn_in['Wg'], 'L0_ffn_w1': _L0_ffn_in['w1'], 'L0_ffn_w3': _L0_ffn_in['w3'], 'L0_ffn_w2': _L0_ffn_in['w2']}

def reference(x, ctx_512, L0_attn_slope_rate, L0_attn_w_qkv, L0_attn_w_gate, L0_attn_w_out, L0_attn_rms_weight, L0_xattn_Wc, L0_xattn_bc, L0_ffn_Wg, L0_ffn_w1, L0_ffn_w3, L0_ffn_w2):
    import jax
    import jax.numpy as jnp

    def _L0_attn_ref(hidden_states, slope_rate, w_qkv, w_gate, w_out, rms_weight):
        import jax, jax.numpy as jnp
        import numpy as np
        B, N, HID, H, D = (2, 1024, 256, 16, 128)
        BLOCK = 32
        EPS = 1e-06

        def _alibi_slopes(h):
            start = 2.0 ** (-2.0 ** (-(np.log2(h) - 3)))
            return np.array([start * start ** i for i in range(h)], dtype=np.float32)

        def _lightning_attention(q, k, v, slope_rate):
            b, h, n, d = q.shape
            nb = n // BLOCK
            s = slope_rate.reshape(1, h, 1, 1).astype(q.dtype)
            arr = jnp.arange(1, BLOCK + 1, dtype=q.dtype)
            q_decay = jnp.exp(-s * arr[None, None, :, None])
            k_decay = jnp.exp(-s * (BLOCK - arr)[None, None, :, None])
            idx = arr[:, None] - arr[None, :]
            diag_decay = jnp.where(idx[None, None] >= 0, jnp.exp(-s * idx[None, None]), 0.0)
            block_decay = jnp.exp(-s * BLOCK)

            def to_blocks(x):
                return x.reshape(b, h, nb, BLOCK, d).transpose(2, 0, 1, 3, 4)
            qb, kb, vb = (to_blocks(q), to_blocks(k), to_blocks(v))

            def step(kv, blk):
                qi, ki, vi = blk
                inter = jnp.einsum('bhld,bhde->bhle', qi * q_decay, kv)
                qk = jnp.einsum('bhld,bhmd->bhlm', qi, ki) * diag_decay
                intra = jnp.einsum('bhlm,bhme->bhle', qk, vi)
                kv = block_decay * kv + jnp.einsum('bhld,bhle->bhde', ki * k_decay, vi)
                return (kv, inter + intra)
            kv0 = jnp.zeros((b, h, d, d), q.dtype)
            _, out = jax.lax.scan(step, kv0, (qb, kb, vb))
            return out.transpose(1, 2, 0, 3, 4).reshape(b, h, n, d)
        b, n, _ = hidden_states.shape
        qkv = jax.nn.silu(hidden_states @ w_qkv)
        q, k, v = jnp.split(qkv, 3, axis=-1)

        def shp(x):
            return x.reshape(b, n, H, D).transpose(0, 2, 1, 3)
        o = _lightning_attention(shp(q), shp(k), shp(v), slope_rate)
        o = o.transpose(0, 2, 1, 3).reshape(b, n, H * D)
        var = jnp.mean(jnp.square(o), axis=-1, keepdims=True)
        o = o * jax.lax.rsqrt(var + EPS) * rms_weight
        o = jax.nn.sigmoid(hidden_states @ w_gate) * o
        return o @ w_out

    def _L0_xattn_ref(q, k, v, Wc, bc):
        import jax, jax.numpy as jnp
        import numpy as np
        import math
        D_MODEL = 256
        N_HEADS = 16
        N_GROUPS = 4
        HEADS_PER_GROUP = N_HEADS // N_GROUPS
        HEAD_DIM = D_MODEL // N_HEADS
        B, S = (2, 256)
        b, s, _ = q.shape
        qh = q.reshape(b, s, N_GROUPS, HEADS_PER_GROUP, HEAD_DIM).transpose(0, 2, 3, 1, 4)
        kh = k.reshape(b, s, N_GROUPS, HEAD_DIM).transpose(0, 2, 1, 3)
        vh = v.reshape(b, s, N_GROUPS, HEAD_DIM).transpose(0, 2, 1, 3)
        scale = 1.0 / math.sqrt(HEAD_DIM)
        scores = jnp.einsum('bghsd,bgtd->bghst', qh, kh) * scale
        probs = jax.nn.softmax(scores, axis=-1)
        out = jnp.einsum('bghst,bgtd->bghsd', probs, vh)
        out = out.transpose(0, 3, 1, 2, 4).reshape(b, s, D_MODEL)
        return out @ Wc.T + bc

    def _L0_ffn_ref(hidden_states, Wg, w1, w3, w2):
        import jax, jax.numpy as jnp
        import numpy as np
        NUM_EXPERTS = 8
        TOP_K = 2
        HIDDEN = 256
        INTER = 704
        B, S = (4, 256)
        orig_shape = hidden_states.shape
        x = hidden_states.reshape(-1, HIDDEN)
        T = x.shape[0]
        router_logits = x @ Wg.T
        probs = jax.nn.softmax(router_logits, axis=-1)
        topk_vals, topk_idx = jax.lax.top_k(probs, TOP_K)
        topk_vals = topk_vals / jnp.sum(topk_vals, axis=-1, keepdims=True)
        combine = jnp.zeros((T, NUM_EXPERTS), dtype=x.dtype)
        combine = combine.at[jnp.arange(T)[:, None], topk_idx].add(topk_vals)
        out = jnp.zeros_like(x)
        for e in range(NUM_EXPERTS):
            h = jax.nn.silu(x @ w1[e].T) * (x @ w3[e].T)
            out = out + combine[:, e:e + 1] * (h @ w2[e].T)
        return out.reshape(orig_shape)
    x = _layernorm(x + _L0_attn_ref(x, L0_attn_slope_rate, L0_attn_w_qkv, L0_attn_w_gate, L0_attn_w_out, L0_attn_rms_weight), axis=-1)
    x = _layernorm(x + _L0_xattn_ref(x, ctx_512, ctx_512, L0_xattn_Wc, L0_xattn_bc), axis=-1)
    x = _layernorm(x + _L0_ffn_ref(x, L0_ffn_Wg, L0_ffn_w1, L0_ffn_w3, L0_ffn_w2), axis=-1)
    return x

_drawn_inputs = setup_inputs


def setup_inputs(seed=0):
    import zlib

    import numpy as np

    out = dict(_drawn_inputs(seed))
    spreads = {'L0_attn_rms_weight': (1.0, 0.2)}
    factors = {}
    for name, (base, spread) in spreads.items():
        noise = np.random.default_rng([zlib.crc32(name.encode()), seed]).standard_normal(out[name].shape)
        drawn = base * np.exp(spread * noise) if base else spread * noise
        out[name] = jnp.asarray(drawn.astype(out[name].dtype))
    for name, factor in factors.items():
        out[name] = (out[name] * factor).astype(out[name].dtype)
    return out
```

```python
from contextlib import ExitStack

import concourse.bass as bass
import concourse.mybir as mybir
from concourse.alu_op_type import AluOpType as ALU

ACT = mybir.ActivationFunctionType
F32 = mybir.dt.float32
F32R = mybir.dt.float32r
I32 = mybir.dt.int32
U32 = mybir.dt.uint32
AX_X = mybir.AxisListType.X

P = 128
BATCHES, SEQ, HID = 16, 64, 256
T = BATCHES * SEQ
KT = HID // P
TT = T // P
H, D = 16, 128
HALF = 512
TH = HALF // P
PAIRS = H // 2
STEPS = 2 * H
GROUPS, HD = 4, 16
XH = GROUPS * 4
CTX = GROUPS * HD
ROWS = 32
NR = P // ROWS
E, INTER = 8, 704
ITILES = -(-INTER // P)
HB = INTER // 2
ITAIL = INTER - (ITILES - 1) * P
SLOTS = 4
MAX_TILES = 2 * T // P + E - 1
EPS_RMS = 1e-6
EPS_LN = 1e-5


def decoder_layer(nc, d):
    with ExitStack() as ctx:
        def sb(name, shape, dt=F32):
            return ctx.enter_context(nc.sbuf_tensor(name, shape, dt))

        def psum(name):
            return ctx.enter_context(nc.psum_tensor(name, [P, 512], F32))

        def sem(name):
            return ctx.enter_context(nc.semaphore(name))

        acc = sb("acc", [P, TT, HID])
        rms_w = sb("rms_w", [P, H])
        slope = sb("slope", [P, H])
        ident = sb("ident", [P, P])
        ones = sb("ones", [P, P])
        before = sb("before", [P, P])
        mhalf = sb("mhalf", [P, TT])
        eps_ln = sb("eps_ln", [P, 1])
        x_rows = sb("x_rows", [P, TT, HID])
        x2 = sb("x2", [P, TT, HID])
        k_all = sb("k_all", [P, BATCHES, 2, P])
        v_all = sb("v_all", [P, BATCHES, GROUPS, 2 * HD])
        wc = sb("wc", [P, KT, HID])
        wg = sb("wg", [P, KT, E])
        bc = sb("bc", [P, HID])
        kx = [sb(f"kx{i}", [P, 2, 2, P]) for i in range(2)]
        vx = [sb(f"vx{i}", [P, 2, GROUPS, 2 * HD]) for i in range(2)]
        z1 = [sb(f"z1_{i}", [P, HID]) for i in range(2)]
        st1 = [sb(f"st1_{i}", [P, 6]) for i in range(2)]
        mv1 = [sb(f"mv1_{i}", [P, 2]) for i in range(2)]
        rs1 = [sb(f"rs1_{i}", [P, 1]) for i in range(2)]
        z2 = [sb(f"z2_{i}", [P, HID]) for i in range(2)]
        st2 = [sb(f"st2_{i}", [P, 6]) for i in range(2)]
        mv2 = [sb(f"mv2_{i}", [P, 2]) for i in range(2)]
        rs2 = [sb(f"rs2_{i}", [P, 1]) for i in range(2)]
        x1 = [sb(f"x1_{i}", [P, HID]) for i in range(2)]
        x1b = [sb(f"x1b_{i}", [P, HID]) for i in range(2)]
        x1T = [sb(f"x1T_{i}", [P, KT, P]) for i in range(2)]
        prob = [sb(f"prob{i}", [P, XH, SEQ]) for i in range(2)]
        pmax = sb("pmax", [P, XH])
        psum_ = [sb(f"psum{i}", [P, XH]) for i in range(2)]
        prec = [sb(f"prec{i}", [P, XH]) for i in range(2)]
        probT = [sb(f"probT{i}", [P, 4, P]) for i in range(2)]
        xo = sb("xo", [P, HID])
        xoT = sb("xoT", [P, KT, P])
        x2s = [sb(f"x2s_{i}", [P, HID]) for i in range(2)]
        x2T = sb("x2T", [P, KT, P])
        logit = sb("logit", [P, TT, E])
        ms = sb("ms", [P, TT])
        zero = sb("zero", [P, HID])
        rank8 = sb("rank8", [P, E])
        steps = sb("steps", [P, TT])
        tile_no = sb("tile_no", [P, MAX_TILES])
        prb = sb("prb", [P, TT, E])
        pick = [sb(f"pick{i}", [P, TT, E]) for i in range(2)]
        cand = sb("cand", [P, TT, E])
        top = sb("top", [P, TT])
        second = sb("second", [P, TT])
        w_top = [sb(f"w_top{i}", [P, TT]) for i in range(2)]
        both = sb("both", [P, TT, E])
        run = [sb(f"run{i}", [P, TT, E]) for i in range(2)]
        more = sb("more", [P, E, TT])
        tiles_of = [sb(f"tiles_of{i}", [P, E]) for i in range(2)]
        end = sb("end", [P, E])
        base = sb("base", [P, E])
        pos = sb("pos", [P, TT, E])
        posx = sb("posx", [P, TT, E])
        slot_f = [sb(f"slot_f{i}", [P, TT]) for i in range(2)]
        slot = [sb(f"slot{i}", [P, TT], U32) for i in range(2)]
        past = sb("past", [P, MAX_TILES, E])
        expert = sb("expert", [P, MAX_TILES])
        upper = sb("upper", [P, MAX_TILES])
        place = sb("place", [P, MAX_TILES], I32)
        need = sb("need", [P, MAX_TILES], I32)
        free_at = sb("free_at", [P, E], I32)
        x_sorted = nc.dram_tensor("x_sorted", (MAX_TILES * P, HID), F32, kind="Internal").ap()
        y_sorted = nc.dram_tensor("y_sorted", (MAX_TILES * P, HID), F32, kind="Internal").ap()
        rms_r = sb("rms_r", [P, TT])

        region = ExitStack()

        def early(name, shape, dt=F32):
            return region.enter_context(nc.sbuf_tensor(name, shape, dt))

        ctx_rows = early("ctx_rows", [P, BATCHES, CTX])
        x_raw = early("x_raw", [P, KT, T])
        xh = early("xh", [P, KT, T], F32R)
        xl = early("xl", [P, KT, T], F32R)
        wa_raw = [early(f"w{a}_raw", [P, KT, 3, D]) for a in range(2)]
        wv_raw = early("wv_raw", [P, KT, 2, D])
        wo_raw = early("wo_raw", [P, 2, HID])
        wa_h = [early(f"w{a}_h", [P, KT, 3, D], F32R) for a in range(2)]
        wa_l = [early(f"w{a}_l", [P, KT, 3, D], F32R) for a in range(2)]
        wv_h = early("wv_h", [P, KT, 2 * D], F32R)
        wv_l = early("wv_l", [P, KT, 2 * D], F32R)
        wo_s = early("wo_s", [P, 2, HID])
        dist = early("dist", [P, P])
        visible = early("visible", [P, P])
        decay = early("decay", [P, H, P])
        qT = [early(f"qT{i}", [P, HALF]) for i in range(2)]
        kT = [early(f"kT{i}", [P, HALF]) for i in range(2)]
        tg = [early(f"tg{i}", [P, HALF]) for i in range(2)]
        pT = [early(f"pT{i}", [P, HALF]) for i in range(2)]
        v_sb = [early(f"v{c}", [P, TH, 2, D]) for c in range(2)]
        go = [early(f"go{a}", [P, T]) for a in range(2)]
        o_sq = [early(f"o_sq{i}", [P, HALF]) for i in range(2)]
        sq_acc = early("sq_acc", [P, T])

        region.close()
        xt_rows = [sb(f"xt_rows{i}", [P, HID]) for i in range(2)]
        xtT = [sb(f"xtT{i}", [P, KT, P]) for i in range(2)]
        act_h = sb("act_h", [P, INTER])
        hid = sb("hid", [P, INTER])
        hidT = [sb(f"hidT{i}", [P, ITILES, P]) for i in range(2)]
        y_rows = [sb(f"y_rows{i}", [P, HID]) for i in range(2)]
        ya = [[sb(f"ya{k}_{i}", [P, HID]) for i in range(2)] for k in range(2)]
        st3 = sb("st3", [P, TT, 6])
        mv3 = sb("mv3", [P, TT, 2])
        rs3 = sb("rs3", [P, TT])
        w13 = sb("w13", [P, SLOTS, KT, 2 * INTER])
        w2 = sb("w2", [P, SLOTS, ITILES, HID])

        sc_all = ctx.enter_context(nc.psum_tensor("ps_qkgv", [P, NR, 512], F32))
        ps_q, ps_k, ps_g, ps_v = (sc_all[:, r, :] for r in range(NR))
        ps_s, ps_o, ps_y0, ps_y1 = (psum(n) for n in ("ps_s", "ps_o", "ps_y0", "ps_y1"))
        ps_y = [ps_y0, ps_y1]

        s_x = sem("x_loaded")
        s_small = sem("small_loaded")
        s_wa = [sem(f"w{a}_loaded") for a in range(2)]
        s_wv = sem("wv_loaded")
        s_wo = sem("wo_loaded")
        s_xs = sem("x_split")
        s_dist = sem("dist_made")
        s_vis = sem("visible_made")
        s_arg_pre = sem("slope_negated")
        s_arg = sem("decay_arg")
        s_exp = sem("decay_exp")
        s_decay = sem("decay_made")
        s_zero = sem("sums_zeroed")
        s_hi = sem("hi_made")
        s_wasp = [sem(f"w{a}_split") for a in range(2)]
        s_wvsp = sem("wv_split")
        s_wosc = sem("wo_scaled")
        s_pq, s_pk, s_pg, s_pv = sem("q_projected"), sem("k_projected"), sem("g_projected"), sem("v_projected")
        s_q, s_k, s_g, s_v = sem("q_ready"), sem("k_ready"), sem("g_ready"), sem("v_ready")
        s_s, s_p, s_o, s_go, s_sq = sem("scores_done"), sem("p_ready"), sem("o_done"), sem("go_ready"), sem("o_squared")
        s_sqa = sem("squares_added")
        s_y = [sem(f"y{i}_done") for i in range(2)]
        s_ya = [sem(f"y{i}_added") for i in range(2)]
        s_out = sem("out_stored")
        s_const = sem("constants_made")
        s_zt, s_xz = sem("zero_tile"), sem("x_sorted_zeroed")
        s_rc = sem("routing_constants")
        s_r = sem("routing_step")
        s_rexp = sem("router_exp")
        s_route_pe = sem("rows_counted")
        s_both = sem("choice_made")
        s_slots = sem("slots_ready")
        s_scat = sem("rows_scattered")
        s_tab = sem("tile_tables")
        s_we = sem("expert_loaded")
        s_xt = [sem(f"tile_loaded{i}") for i in range(2)]
        s_tt, s_tT = sem("tile_turned"), sem("tileT_ready")
        s_h = [sem(f"hidden_done{i}") for i in range(2)]
        s_si = [sem(f"silu_done{i}") for i in range(2)]
        s_hm = [sem(f"hidden_ready{i}") for i in range(2)]
        s_ht, s_hT = sem("hidden_turned"), [sem(f"hiddenT_ready{i}") for i in range(2)]
        s_yd, s_yr = sem("one_and_tiles_finished"), sem("y_copied")
        s_yst = [sem(f"y_stored{i}") for i in range(2)]
        s_ga = [sem(f"gathered{i}") for i in range(2)]
        s_c1, s_c2, s_c3, s_c4 = sem("added_first"), sem("added_second"), sem("bn3"), sem("mv3")
        s_e3, s_r3, s_x3 = sem("eps3"), sem("rstd3"), sem("x3_ready")
        s_cm = sem("constants_filled")
        s_xr = sem("x_rows_loaded")
        s_kz, s_vz = sem("k_zeroed"), sem("v_zeroed")
        s_kl, s_cl, s_wl = sem("k_loaded"), sem("ctx_loaded"), sem("cross_weights_loaded")
        s_va = sem("v_arranged")
        s_pms, s_ms, s_rms = sem("squares_summed"), sem("mean_square"), sem("rms_ready")
        s_pms2 = sem("mean_square_eps")
        s_z1, s_b1, s_m1, s_e1, s_r1 = sem("z1"), sem("bn1"), sem("mv1"), sem("eps1"), sem("rstd1")
        s_x1, s_x1b = sem("x1_ready"), sem("x1_plus_bias")
        s_z2, s_b2, s_m2, s_e2, s_r2 = sem("z2"), sem("bn2"), sem("mv2"), sem("eps2"), sem("rstd2")
        s_x2, s_x2c = sem("x2_ready"), sem("x2_kept")
        s_x1t, s_x1T = sem("x1_turned"), sem("x1T_ready")
        s_kx, s_vx = sem("kx_ready"), sem("vx_ready")
        s_xs_, s_mx, s_sub, s_pe = sem("cross_scores"), sem("row_max"), sem("max_off"), sem("exp_done")
        s_ps, s_pr = sem("prob_sum"), sem("sum_inverse")
        s_pt, s_pT = [sem(f"prob_turned{i}") for i in range(2)], [sem(f"probT_ready{i}") for i in range(2)]
        s_pvx, s_xo = sem("cross_values"), sem("xo_ready")
        s_xot, s_xoT, s_wcd = sem("xo_turned"), sem("xoT_ready"), sem("wc_done")
        s_x2t, s_x2T, s_rt, s_lg = sem("x2_turned"), sem("x2T_ready"), sem("router_done"), sem("logits_ready")

        ps_sc = [ps_q, ps_k, ps_g, ps_v]
        ps_pt = [ps_s, ps_o]
        ps_x1, ps_x = ps_y0, ps_y1

        block = ctx.enter_context(nc.Block())

        def cross_steps(loop, stage):
            for p in (-2, -1, 0):
                stage(p, p % 2)
            with loop(1, 4, 2) as p:
                stage(p, 1)
                stage(p + 1, 0)
            for p in (5, 6, 7, 8):
                stage(p, p % 2)

        def has(p, lag):
            return not isinstance(p, int) or 0 <= p + lag < TT

        def at_least(p, n):
            return not isinstance(p, int) or p >= n

        def expert_steps(loop, stage):
            for i in (-1, 0):
                stage(i, i % 2)
            last = 1 + (MAX_TILES - 3) // 2 * 2
            with loop(1, last - 1, 2) as i:
                stage(i, 1)
                stage(i + 1, 0)
            for i in range(last, MAX_TILES + 1):
                stage(i, i % 2)

        def tile_exists(i, lag):
            return not isinstance(i, int) or 0 <= i + lag < MAX_TILES

        def one(t, i):
            return t[0:1, i:i + 1] if isinstance(i, int) else t[0:1, bass.ds(i, 1)]

        def rows_of(t, i):
            return t[i * P:(i + 1) * P, :] if isinstance(i, int) else t[bass.ds(i * P, P), :]

        def tile(t, p):
            return t[:, p:p + 1, :] if isinstance(p, int) else t[:, bass.ds(p, 1), :]

        @block.sync
        def _(sp):
            def load_pair(i, first):
                if not first:
                    sp.wait_ge(s_wasp[0], i)
                sp.dma_start(wa_raw[0][:, :, :, :], d["wa"][2 * i]).then_inc(s_wa[0], 16)
                if not first:
                    sp.wait_ge(s_wvsp, i)
                sp.dma_start(wv_raw[:, :, :, :], d["wv"][i]).then_inc(s_wv, 16)
                if not first:
                    sp.wait_ge(s_wosc, i)
                sp.dma_start(wo_raw[:, :, :], d["wo"][i]).then_inc(s_wo, 16)
                if not first:
                    sp.wait_ge(s_wasp[1], i)
                sp.dma_start(wa_raw[1][:, :, :, :], d["wa"][2 * i + 1]).then_inc(s_wa[1], 16)

            sp.dma_start(x_raw[:, :, :], d["xT"].rearrange("(k p) t -> p k t", p=P)).then_inc(s_x, 16)
            load_pair(0, True)
            sp.dma_start(slope[:, :], d["slope"].to_broadcast([P, H])).then_inc(s_small, 16)
            sp.dma_start(rms_w[:, :], d["rms"]).then_inc(s_small, 16)
            with sp.Fori(1, PAIRS) as i:
                load_pair(i, False)
            sp.dma_start(x_rows[:, :, :], d["x"].rearrange("(t p) n -> p t n", p=P)).then_inc(s_xr, 16)
            for hh in range(2):
                sp.dma_start(ctx_rows[hh * SEQ:(hh + 1) * SEQ, :, :],
                             d["ctx"].rearrange("(b t) d -> t b d", t=SEQ)).then_inc(s_cl, 16)
            sp.wait_ge(s_kz, 1)
            for r in range(NR):
                for hh in range(2):
                    for f in range(2):
                        p0, g = r * ROWS + hh * HD, 2 * f + r // 2
                        sp.dma_start(k_all[p0:p0 + HD, :, f, hh * SEQ:(hh + 1) * SEQ],
                                     d["ctxT"][g * HD:(g + 1) * HD, :].rearrange("d (b t) -> d b t", t=SEQ)
                                     ).then_inc(s_kl, 16)
            sp.dma_start(wc[:, :, :], d["wcT"].rearrange("(k p) n -> p k n", p=P)).then_inc(s_wl, 16)
            sp.dma_start(wg[:, :, :], d["wgT"].rearrange("(k p) n -> p k n", p=P)).then_inc(s_wl, 16)
            sp.dma_start(bc[:, :], d["bc"].to_broadcast([P, HID])).then_inc(s_wl, 16)
            sp.wait_ge(s_zt, 1)
            sp.dma_start(x_sorted.rearrange("(t p) n -> p t n", p=P),
                         zero[:, None, :].to_broadcast([P, MAX_TILES, HID])).then_inc(s_xz, 16)

            def load_expert(e):
                for dst, src in ((w13[:, e % SLOTS, :, :], d["w13"][e]),
                                 (w2[:, e % SLOTS, 0:ITILES - 1, :], d["w2a"][e]),
                                 (w2[0:ITAIL, e % SLOTS, ITILES - 1, :], d["w2b"][e])):
                    sp.dma_start(dst, src).then_inc(s_we, 16)
                sp.wait_ge(s_we, 48 * (e + 1))

            sp.wait_ge(s_pms, 1)
            for e in range(SLOTS):
                load_expert(e)
            sp.wait_ge(s_tab, 1)
            for e in range(SLOTS, E):
                ready = sp.value_load(free_at[0:1, e - SLOTS:e - SLOTS + 1], min_val=1, max_val=MAX_TILES + 1)
                sp.wait_ge(s_yd, ready)
                load_expert(e)
            for half in range(2):
                ts = slice(half * TT // 2, (half + 1) * TT // 2)
                sp.wait_ge(s_x3, (half + 1) * TT // 2)
                sp.dma_start(d["out"].rearrange("(t p) n -> p t n", p=P)[:, ts, :], acc[:, ts, :]).then_inc(s_out, 16)
            sp.wait_ge(s_out, 32)

        @block.scalar
        def _(act):
            act.wait_ge(s_arg, 1)
            nc.scalar.activation(decay[:, :, :], decay[:, :, :], ACT.Exp).then_inc(s_exp, 1)

            def values(n_v, c, part, wait_free, it):
                act.wait_ge(s_pv, n_v + 1)
                if wait_free:
                    act.wait_ge(s_o, 4 * it - 1 + c)
                nc.scalar.activation(v_sb[c][:, 2 * part:2 * part + 2, :, :],
                                     ps_v[:, :].rearrange("p (j a e) -> p j a e", j=2, a=2),
                                     ACT.Silu).then_inc(s_v, 1)

            def step(it, s, first):
                n = 4 * it + s
                par = s % 2
                act.wait_ge(s_pq, n + 1)
                if not (first and s < 2):
                    act.wait_ge(s_s, n - 1)
                nc.scalar.activation(qT[par][:, :], ps_q[:, :], ACT.Silu).then_inc(s_q, 1)
                if s < 2:
                    values(4 * it + 2 * s, s, 0, not first, it)
                act.wait_ge(s_pk, n + 1)
                nc.scalar.activation(kT[par][:, :], ps_k[:, :], ACT.Silu).then_inc(s_k, 1)
                if s < 2:
                    values(4 * it + 2 * s + 1, s, 1, False, it)
                if not (first and s == 0):
                    act.wait_ge(s_go, n)
                    if not (first and s < 3):
                        act.wait_ge(s_sqa, n - 2)
                    nc.scalar.activation(o_sq[1 - par][:, :], ps_o[:, :], ACT.Square).then_inc(s_sq, 1)
                act.wait_ge(s_pg, n + 1)
                nc.scalar.activation(tg[par][:, :], ps_g[:, :], ACT.Tanh, scale=0.5).then_inc(s_g, 1)

            for s in range(4):
                step(0, s, True)
            with act.Fori(1, PAIRS) as it:
                for s in range(4):
                    step(it, s, False)
            act.wait_ge(s_go, STEPS)
            act.wait_ge(s_sqa, STEPS - 2)
            nc.scalar.activation(o_sq[(STEPS - 1) % 2][:, :], ps_o[:, :], ACT.Square).then_inc(s_sq, 1)

            def cross(p, par):
                nxt = 1 - par
                if has(p, 0):
                    for b in range(2):
                        act.wait_ge(s_pt[b], p + 1)
                        if at_least(p, 1):
                            act.wait_ge(s_pvx, p)
                        nc.scalar.activation(probT[b][:, :, :].rearrange("p j t -> p (j t)"),
                                             ps_pt[b][:, :], ACT.Copy).then_inc(s_pT[b], 1)
                if has(p, 1):
                    act.wait_ge(s_x1t, p + 2)
                    if at_least(p, 1):
                        act.wait_ge(s_xs_, p)
                    nc.scalar.activation(x1T[nxt][:, :, :].rearrange("p k t -> p (k t)"),
                                         ps_x1[:, 0:HID], ACT.Copy, scale=HD ** -0.5).then_inc(s_x1T, 1)
                if has(p, -1):
                    act.wait_ge(s_x2t, p)
                    if at_least(p, 2):
                        act.wait_ge(s_rt, p - 1)
                    nc.scalar.activation(x2T[:, :, :].rearrange("p k t -> p (k t)"),
                                         ps_x1[:, 0:HID], ACT.Copy).then_inc(s_x2T, 1)
                if has(p, 1):
                    act.wait_ge(s_sub, 2 * p + 4)
                    pr = prob[nxt][:, :, :].rearrange("p h t -> p (h t)")
                    nc.scalar.activation(pr, pr, ACT.Exp).then_inc(s_pe, 1)
                if has(p, 0):
                    act.wait_ge(s_xot, p + 1)
                    if at_least(p, 1):
                        act.wait_ge(s_wcd, p)
                    nc.scalar.activation(xoT[:, :, :].rearrange("p k t -> p (k t)"),
                                         ps_x[:, 0:HID], ACT.Copy).then_inc(s_xoT, 1)

            cross_steps(act.Fori, cross)
            act.wait_ge(s_r, 2)
            nc.scalar.activation(prb[:, :, :], prb[:, :, :], ACT.Exp).then_inc(s_rexp, 1)

            act.wait_ge(s_scat, 2 * TT * 16)

            def load_tile(i, par):
                act.dma_start(xt_rows[par][:, :], rows_of(x_sorted, i)).then_inc(s_xt[par], 16)

            load_tile(0, 0)
            load_tile(1, 1)

            def expert(i, par):
                nxt = 1 - par
                if tile_exists(i, 0) and tile_exists(i, 2):
                    act.wait_ge(s_tt, i + 1)
                    load_tile(i + 2, par)
                if tile_exists(i, 0):
                    for c in range(2):
                        act.wait_ge(s_h[c], i + 1)
                        if at_least(i, 1):
                            act.wait_ge(s_hm[c], i)
                        nc.scalar.activation(act_h[:, c * HB:(c + 1) * HB], sc_all[:, 2 * c, 0:HB], ACT.Silu
                                             ).then_inc(s_si[c], 1)
                if tile_exists(i, 1):
                    act.wait_ge(s_tt, i + 2)
                    if at_least(i, 1):
                        act.wait_ge(s_h[1], i)
                    nc.scalar.activation(xtT[nxt][:, :, :].rearrange("p k t -> p (k t)"), ps_x1[:, 0:HID], ACT.Copy
                                         ).then_inc(s_tT, 1)
                if tile_exists(i, 0):
                    act.wait_ge(s_ht, i + 1)
                    if at_least(i, 2):
                        act.wait_ge(s_yd, i)
                    nc.scalar.activation(hidT[par][:, 0:4, :].rearrange("p k t -> p (k t)"), ps_s[:, :], ACT.Copy
                                         ).then_inc(s_hT[0], 1)

            expert_steps(act.Fori, expert)

        @block.gpsimd
        def _(pool):
            nc.gpsimd.iota(dist[:, :], pattern=[[1, P]], base=0, channel_multiplier=-1,
                           allow_small_or_imprecise_dtypes=True).then_inc(s_dist, 1)
            nc.gpsimd.memset(visible[:, :], 1.0).then_inc(s_vis, 1)
            pool.wait_ge(s_vis, 1)
            nc.gpsimd.affine_select(out=visible[:, :], in_=visible[:, :], compare_op=ALU.is_ge, fill=0.0,
                                    base=0, pattern=[[1, P]], channel_multiplier=-1).then_inc(s_vis, 1)
            pool.wait_ge(s_vis, 2)
            nc.gpsimd.memset(visible[0:SEQ, SEQ:P], 0.0).then_inc(s_vis, 1)
            pool.wait_ge(s_dist, 1)
            pool.wait_ge(s_vis, 3)
            nc.gpsimd.tensor_tensor(dist[:, :], dist[:, :], visible[:, :], ALU.mult).then_inc(s_dist, 1)
            nc.gpsimd.memset(sq_acc[:, :], 0.0).then_inc(s_zero, 1)
            nc.gpsimd.memset(acc[:, :, :], 0.0).then_inc(s_zero, 1)
            pool.wait_ge(s_zero, 1)

            def add_squares(n, s):
                c = s % 2
                half = sq_acc[:, c * HALF:(c + 1) * HALF]
                pool.wait_ge(s_sq, n + 1)
                if not isinstance(n, int) or n >= 2:
                    pool.wait_ge(s_sqa, n - 1)
                nc.gpsimd.tensor_tensor(half, half, o_sq[s % 2][:, :], ALU.add).then_inc(s_sqa, 1)

            for s in range(4):
                add_squares(s, s)
            nc.gpsimd.memset(k_all[:, :, :, :], 0.0).then_inc(s_kz, 1)
            nc.gpsimd.memset(v_all[:, :, :, :], 0.0).then_inc(s_vz, 1)
            nc.gpsimd.memset(zero[:, :], 0.0).then_inc(s_zt, 1)
            nc.gpsimd.iota(rank8[:, :], pattern=[[-1, E]], base=E, channel_multiplier=0,
                           allow_small_or_imprecise_dtypes=True).then_inc(s_rc, 1)
            nc.gpsimd.iota(steps[:, :], pattern=[[P, TT]], base=0, channel_multiplier=0,
                           allow_small_or_imprecise_dtypes=True).then_inc(s_rc, 1)
            nc.gpsimd.iota(tile_no[:, :], pattern=[[1, MAX_TILES]], base=0, channel_multiplier=0,
                           allow_small_or_imprecise_dtypes=True).then_inc(s_rc, 1)
            nc.gpsimd.memset(ident[:, :], 0.0).then_inc(s_cm, 1)
            nc.gpsimd.memset(ones[:, :], 1.0).then_inc(s_cm, 1)
            nc.gpsimd.memset(mhalf[:, :], -0.5).then_inc(s_const, 1)
            nc.gpsimd.memset(eps_ln[:, :], EPS_LN).then_inc(s_const, 1)
            pool.wait_ge(s_cm, 2)
            nc.gpsimd.affine_select(out=ident[:, :], in_=ident[:, :], compare_op=ALU.not_equal, fill=1.0,
                                    base=0, pattern=[[-1, P]], channel_multiplier=1).then_inc(s_const, 1)
            nc.gpsimd.affine_select(out=before[:, :], in_=ones[:, :], compare_op=ALU.is_gt, fill=0.0,
                                    base=0, pattern=[[1, P]], channel_multiplier=-1).then_inc(s_const, 1)
            with pool.Fori(1, PAIRS) as it:
                for s in range(4):
                    add_squares(4 * it + s, s)
            pool.wait_ge(s_vz, 1)
            pool.wait_ge(s_cl, 32)
            for hh in range(2):
                rows = slice(hh * SEQ, (hh + 1) * SEQ)
                pool.wait_ge(s_va, 1) if hh else pool.wait_ge(s_sqa, STEPS)
                nc.gpsimd.tensor_copy(v_all[rows, :, :, hh * HD:(hh + 1) * HD],
                                      ctx_rows[rows, :, :].rearrange("p b (g d) -> p b g d", g=GROUPS)
                                      ).then_inc(s_va, 1)

            def inv_root(out, var, eps_ready, done, count, eps):
                if eps is not None:
                    nc.gpsimd.tensor_tensor(var, var, eps, ALU.add).then_inc(eps_ready, 1)
                    pool.wait_ge(eps_ready, count)
                nc.gpsimd.tensor_tensor(out, var, mhalf[:, 0:out.shape[1]], ALU.pow).then_inc(done, 1)

            pool.wait_ge(s_const, 4)
            pool.wait_ge(s_ms, 1)
            pool.wait_ge(s_va, 2)
            inv_root(rms_r[:, :], ms[:, :], None, s_rms, 1, None)
            pool.wait_ge(s_wl, 48)

            def cross(p, par):
                nxt = 1 - par
                if has(p, 2):
                    pool.wait_ge(s_m1, p + 3)
                    inv_root(rs1[par][:, :], mv1[par][:, 1:2], s_e1, s_r1, p + 3, eps_ln[:, :])
                    pool.wait_ge(s_x1, p + 3)
                    if at_least(p, 0):
                        pool.wait_ge(s_z2, p + 1)
                    nc.gpsimd.tensor_tensor(x1b[par][:, :], x1[par][:, :], bc[:, :], ALU.add).then_inc(s_x1b, 1)
                if has(p, 0):
                    pool.wait_ge(s_m2, p + 1)
                    inv_root(rs2[par][:, :], mv2[par][:, 1:2], s_e2, s_r2, p + 1, eps_ln[:, :])
                    pool.wait_ge(s_x2, p + 1)
                    nc.gpsimd.tensor_copy(tile(x2, p), x2s[par][:, :]).then_inc(s_x2c, 1)

            cross_steps(pool.Fori, cross)

            pool.wait_ge(s_slots, 1)
            pool.wait_ge(s_xz, 16)
            pool.wait_ge(s_x2c, TT)
            for k in range(2):
                for t in range(TT):
                    pool.indirect_dma_start(
                        out=x_sorted, out_offset=bass.IndirectOffsetOnAxis(ap=slot[k][:, t:t + 1], axis=0),
                        in_=x2[:, t, :], in_offset=None).then_inc(s_scat, 16)

            def store(i, par):
                if tile_exists(i, -1):
                    pool.wait_ge(s_yr, i)
                    pool.dma_start(rows_of(y_sorted, i - 1), y_rows[1 - par][:, :]).then_inc(s_yst[1 - par], 16)

            expert_steps(pool.Fori, store)
            pool.wait_ge(s_yst[0], 16 * ((MAX_TILES + 1) // 2))
            pool.wait_ge(s_yst[1], 16 * (MAX_TILES // 2))
            for t in range(TT):
                if t >= 2:
                    pool.wait_ge(s_c2, t - 1)
                for k in range(2):
                    pool.indirect_dma_start(
                        out=ya[k][t % 2][:, :], out_offset=None, in_=y_sorted,
                        in_offset=bass.IndirectOffsetOnAxis(ap=slot[k][:, t:t + 1], axis=0)
                    ).then_inc(s_ga[t % 2], 16)
                if t % (TT // 2) == TT // 2 - 1:
                    half = t // (TT // 2)
                    ts = slice(half * TT // 2, (half + 1) * TT // 2)
                    pool.wait_ge(s_c4, t + 1)
                    inv_root(rs3[:, ts], mv3[:, ts, 1], s_e3, s_r3, half + 1,
                             eps_ln[:, :].to_broadcast([P, TT // 2]))

        @block.vector
        def _(dve):
            hi = [0]

            dve.wait_ge(s_x, 16)
            nc.vector.tensor_copy(xh[:, :, :], x_raw[:, :, :]).then_inc(s_hi, 1)
            dve.wait_ge(s_hi, 1)
            nc.vector.tensor_tensor(xl[:, :, :], x_raw[:, :, :], xh[:, :, :], ALU.subtract).then_inc(s_xs, 1)

            def split_a(i, a, base):
                dve.wait_ge(s_wa[a], 16 * i + 16)
                nc.vector.tensor_copy(wa_h[a][:, :, :, :], wa_raw[a][:, :, :, :]).then_inc(s_hi, 1)
                dve.wait_ge(s_hi, base)
                nc.vector.tensor_tensor(wa_l[a][:, :, :, :], wa_raw[a][:, :, :, :], wa_h[a][:, :, :, :],
                                        ALU.subtract).then_inc(s_wasp[a], 1)

            def split_v(i, base):
                raw = wv_raw[:, :, :, :].rearrange("p k a e -> p k (a e)")
                dve.wait_ge(s_wv, 16 * i + 16)
                nc.vector.tensor_copy(wv_h[:, :, :], raw).then_inc(s_hi, 1)
                dve.wait_ge(s_hi, base)
                nc.vector.tensor_tensor(wv_l[:, :, :], raw, wv_h[:, :, :], ALU.subtract).then_inc(s_wvsp, 1)

            split_a(0, 0, 2)
            split_v(0, 3)
            dve.wait_ge(s_small, 32)
            dve.wait_ge(s_dist, 2)
            nc.vector.tensor_scalar(slope[:, :], slope[:, :], -1.0, None, ALU.mult).then_inc(s_arg_pre, 1)
            dve.wait_ge(s_arg_pre, 1)
            nc.vector.tensor_tensor(decay[:, :, :], dist[:, None, :].to_broadcast([P, H, P]),
                                    slope[:, :, None].to_broadcast([P, H, P]), ALU.mult).then_inc(s_arg, 1)
            dve.wait_ge(s_exp, 1)
            nc.vector.tensor_tensor(decay[:, :, :], decay[:, :, :],
                                    visible[:, None, :].to_broadcast([P, H, P]), ALU.mult).then_inc(s_decay, 1)

            def mask(m, s, it_of, early):
                dve.wait_ge(s_s, m + 1)
                if not early:
                    dve.wait_ge(s_o, m - 1)
                a = s // 2
                head = decay[:, bass.ds(2 * it_of + a, 1), :] if not isinstance(it_of, int) \
                    else decay[:, 2 * it_of + a:2 * it_of + a + 1, :]
                nc.vector.tensor_tensor(pT[s % 2][:, :].rearrange("p (j i) -> p j i", j=TH),
                                        ps_s[:, :].rearrange("p (j i) -> p j i", j=TH),
                                        head.to_broadcast([P, TH, P]), ALU.mult).then_inc(s_p, 1)

            def gate(m, s):
                a, c = s // 2, s % 2
                dve.wait_ge(s_o, m + 1)
                dve.wait_ge(s_g, m + 1)
                nc.vector.scalar_tensor_tensor(out=go[a][:, c * HALF:(c + 1) * HALF], in0=tg[s % 2][:, :],
                                               scalar=1.0, in1=ps_o[:, :], op0=ALU.add, op1=ALU.mult
                                               ).then_inc(s_go, 1)

            def add_out(i, c):
                for b in range(2):
                    dve.wait_ge(s_y[b], 2 * i + c + 1)
                    part = acc[:, TH * c + 2 * b:TH * c + 2 * b + 2, :].rearrange("p t n -> p (t n)")
                    nc.vector.tensor_tensor(part, part, ps_y[b][:, :], ALU.add).then_inc(s_ya[b], 1)

            def step(it, s, first):
                n = 4 * it + s
                last_it = it - 1 if s == 0 else it
                if not (first and s == 0):
                    mask(n - 1, (s - 1) % 4, last_it, first and s < 3)
                if s == 0:
                    if not first:
                        dve.wait_ge(s_pg, n)
                    split_a(it, 1, 3 * it + 4)
                if not (first and s == 0):
                    if not first and s in (1, 2):
                        dve.wait_ge(s_y[1], 2 * it - 1 + s - 1)
                    gate(n - 1, (s - 1) % 4)
                if s < 2 and not first:
                    add_out(it - 1, s)

            def scale_out(it):
                dve.wait_ge(s_wo, 16 * it + 16)
                for a in range(2):
                    r = rms_w[:, 2 * it + a:2 * it + a + 1] if isinstance(it, int) \
                        else rms_w[:, bass.ds(2 * it + a, 1)]
                    ins = nc.vector.tensor_scalar(wo_s[:, a, :], wo_raw[:, a, :], r, 0.5, ALU.mult, ALU.mult)
                ins.then_inc(s_wosc, 1)

            def pair(it, first, last):
                for s in range(4):
                    step(it, s, first)
                    if s == 0 and first:
                        dve.wait_ge(s_zero, 2)
                    if s == 2:
                        if not last:
                            dve.wait_ge(s_pg, 4 * it + 2)
                            split_a(it + 1, 0, 3 * it + 5)
                        scale_out(it)
                    if s == 3 and not last:
                        dve.wait_ge(s_pv, 4 * it + 4)
                        split_v(it + 1, 3 * it + 6)

            pair(0, True, False)
            with dve.Fori(1, PAIRS - 1) as it:
                pair(it, False, False)
            pair(PAIRS - 1, False, True)
            mask(STEPS - 1, 3, PAIRS - 1, False)
            add_out(PAIRS - 1, 0)
            gate(STEPS - 1, 3)
            add_out(PAIRS - 1, 1)

            dve.wait_ge(s_pms, 1)
            nc.vector.tensor_scalar(ms[:, :], ps_x[:, 0:TT], 1.0 / (H * D), EPS_RMS, ALU.mult, ALU.add
                                    ).then_inc(s_ms, 1)
            dve.wait_ge(s_xr, 16)
            dve.wait_ge(s_va, 2)
            dve.wait_ge(s_kl, 16 * 16)
            dve.wait_ge(s_rms, 1)
            for b in range(2):
                dve.wait_ge(s_ya[b], 2 * PAIRS)

            def cross(p, par):
                nxt = 1 - par
                if has(p, 2):
                    r = rms_r[:, p + 2:p + 3] if isinstance(p, int) else rms_r[:, bass.ds(p + 2, 1)]
                    nc.vector.scalar_tensor_tensor(out=z1[par][:, :], in0=tile(acc, p + 2)[:, 0, :]
                                                   if isinstance(p, int) else tile(acc, p + 2).rearrange("p a n -> p (a n)"),
                                                   scalar=r, in1=tile(x_rows, p + 2).rearrange("p a n -> p (a n)"),
                                                   op0=ALU.mult, op1=ALU.add).then_inc(s_z1, 1)
                    dve.wait_ge(s_z1, p + 3)
                    nc.vector.bn_stats(st1[par][:, :], z1[par][:, :]).then_inc(s_b1, 1)
                    dve.wait_ge(s_b1, p + 3)
                if has(p, 1):
                    if at_least(p, 1):
                        dve.wait_ge(s_xs_, p)
                    src = k_all[:, 2 * p + 2:2 * p + 4, :, :] if isinstance(p, int) \
                        else k_all[:, bass.ds(2 * p + 2, 2), :, :]
                    nc.vector.tensor_copy(kx[nxt][:, :, :, :], src).then_inc(s_kx, 1)
                if has(p, 2):
                    nc.vector.bn_aggr(mv1[par][:, :], st1[par][:, :]).then_inc(s_m1, 1)
                if has(p, 1):
                    if at_least(p, 1):
                        dve.wait_ge(s_pvx, p)
                    src = v_all[:, 2 * p + 2:2 * p + 4, :, :] if isinstance(p, int) \
                        else v_all[:, bass.ds(2 * p + 2, 2), :, :]
                    nc.vector.tensor_copy(vx[nxt][:, :, :, :], src).then_inc(s_vx, 1)
                if has(p, 2):
                    dve.wait_ge(s_r1, p + 3)
                    if at_least(p, 0):
                        dve.wait_ge(s_x1b, p + 1)
                        dve.wait_ge(s_x1t, p + 1)
                    nc.vector.tensor_scalar(x1[par][:, :], z1[par][:, :], mv1[par][:, 0:1], rs1[par][:, 0:1],
                                            ALU.subtract, ALU.mult).then_inc(s_x1, 1)
                if has(p, 0):
                    dve.wait_ge(s_pvx, p + 1)
                    dve.wait_ge(s_pr, p + 1)
                    if at_least(p, 1):
                        dve.wait_ge(s_xot, p)
                    for b in range(2):
                        rows = slice(b * SEQ, (b + 1) * SEQ)
                        src = ps_x[:, :].rearrange("p (j b h d) -> p j b h d", b=2, h=2, d=HD)[rows, :, b, :, :]
                        nc.vector.tensor_tensor(
                            xo[rows, :].rearrange("p (j h d) -> p j h d", h=2, d=HD), src,
                            prec[par][rows, :].rearrange("p (j h) -> p j h", h=2)[:, :, :, None]
                            .to_broadcast([SEQ, XH // 2, 2, HD]), ALU.mult).then_inc(s_xo, 1)
                if has(p, 1):
                    dve.wait_ge(s_xs_, p + 2)
                    nc.vector.tensor_reduce(pmax[:, :].rearrange("p (r c) -> p r c", r=NR),
                                            sc_all[:, :, 0:2 * P].rearrange("p r (c t) -> p r c t", t=SEQ),
                                            AX_X, ALU.max).then_inc(s_mx, 1)
                    dve.wait_ge(s_mx, p + 2)
                    if at_least(p, 1):
                        dve.wait_ge(s_pt[1], p)
                    for f in range(2):
                        nc.vector.tensor_tensor(
                            prob[nxt][:, 8 * f:8 * f + 8, :].rearrange("p (r h) t -> p r h t", r=NR),
                            sc_all[:, :, f * P:(f + 1) * P].rearrange("p r (h t) -> p r h t", h=2),
                            pmax[:, :].rearrange("p (r f h) -> p r f h", r=NR, f=2)[:, :, f, :, None]
                            .to_broadcast([P, NR, 2, SEQ]), ALU.subtract).then_inc(s_sub, 1)
                if has(p, 0):
                    dve.wait_ge(s_wcd, p + 1)
                    dve.wait_ge(s_x1b, p + 1)
                    nc.vector.tensor_tensor(z2[par][:, :], ps_x[:, 0:HID], x1b[par][:, :], ALU.add
                                            ).then_inc(s_z2, 1)
                    dve.wait_ge(s_z2, p + 1)
                    nc.vector.bn_stats(st2[par][:, :], z2[par][:, :]).then_inc(s_b2, 1)
                    dve.wait_ge(s_b2, p + 1)
                if has(p, 1):
                    dve.wait_ge(s_pe, p + 2)
                    nc.vector.tensor_reduce(psum_[nxt][:, :], prob[nxt][:, :, :], AX_X, ALU.add).then_inc(s_ps, 1)
                if has(p, 0):
                    nc.vector.bn_aggr(mv2[par][:, :], st2[par][:, :]).then_inc(s_m2, 1)
                if has(p, 1):
                    dve.wait_ge(s_ps, p + 2)
                    nc.vector.reciprocal(prec[nxt][:, :], psum_[nxt][:, :]).then_inc(s_pr, 1)
                if has(p, 0):
                    dve.wait_ge(s_r2, p + 1)
                    if at_least(p, 2):
                        dve.wait_ge(s_x2c, p - 1)
                        dve.wait_ge(s_x2t, p - 1)
                    nc.vector.tensor_scalar(x2s[par][:, :], z2[par][:, :], mv2[par][:, 0:1], rs2[par][:, 0:1],
                                            ALU.subtract, ALU.mult).then_inc(s_x2, 1)
                if has(p, -1):
                    dve.wait_ge(s_rt, p)
                    nc.vector.tensor_copy(tile(logit, p - 1), ps_x1[:, 256:256 + E]).then_inc(s_lg, 1)

            cross_steps(dve.Fori, cross)

            done = [0]

            def step_done(ins):
                done[0] += 1
                ins.then_inc(s_r, 1)
                dve.wait_ge(s_r, done[0])

            def over_experts(t):
                return t[:, :, None].to_broadcast([P, TT, E])

            tt, tred = nc.vector.tensor_tensor, nc.vector.tensor_reduce
            dve.wait_ge(s_lg, TT)
            dve.wait_ge(s_rc, 3)
            step_done(tred(top[:, :], logit[:, :, :], AX_X, ALU.max))
            step_done(tt(prb[:, :, :], logit[:, :, :], over_experts(top), ALU.subtract))
            dve.wait_ge(s_rexp, 1)

            def choose(k, best):
                step_done(tred(best[:, :], prb[:, :, :], AX_X, ALU.max))
                step_done(tt(cand[:, :, :], prb[:, :, :], over_experts(best), ALU.is_equal))
                step_done(tt(cand[:, :, :], cand[:, :, :], rank8[:, None, :].to_broadcast([P, TT, E]), ALU.mult))
                step_done(tred(slot_f[k][:, :], cand[:, :, :], AX_X, ALU.max))
                step_done(tt(pick[k][:, :, :], cand[:, :, :], over_experts(slot_f[k]), ALU.is_equal))

            choose(0, top)
            step_done(nc.vector.scalar_tensor_tensor(out=prb[:, :, :], in0=pick[0][:, :, :], scalar=-2.0,
                                                     in1=prb[:, :, :], op0=ALU.mult, op1=ALU.add))
            choose(1, second)
            step_done(tt(both[:, :, :], pick[0][:, :, :], pick[1][:, :, :], ALU.add))
            nc.vector.tensor_copy(run[0][:, :, :], both[:, :, :]).then_inc(s_both, 1)
            step_done(tt(w_top[1][:, :], top[:, :], second[:, :], ALU.add))
            step_done(nc.vector.reciprocal(w_top[1][:, :], w_top[1][:, :]))
            step_done(tt(w_top[0][:, :], w_top[1][:, :], top[:, :], ALU.mult))
            step_done(tt(w_top[1][:, :], w_top[1][:, :], second[:, :], ALU.mult))
            dve.wait_ge(s_route_pe, 1)
            counts = ps_s[:, 64:64 + TT * E].rearrange("p (t e) -> p t e", e=E)
            step_done(nc.vector.tensor_copy(run[0][:, :, :], counts))
            src = 0
            for hop in (1, 2, 4):
                a, b = run[src], run[1 - src]
                nc.vector.tensor_copy(b[:, 0:hop, :], a[:, 0:hop, :])
                step_done(tt(b[:, hop:, :], a[:, hop:, :], a[:, 0:TT - hop, :], ALU.add))
                src = 1 - src
            total = run[src][:, TT - 1, :]
            step_done(tt(more[:, :, :], total[:, :, None].to_broadcast([P, E, TT]),
                         steps[:, None, :].to_broadcast([P, E, TT]), ALU.is_gt))
            step_done(tred(tiles_of[0][:, :], more[:, :, :], AX_X, ALU.add))
            step_done(nc.vector.tensor_copy(base[:, :], tiles_of[0][:, :]))
            cur = 0
            for hop in (1, 2, 4):
                a, b = tiles_of[cur], tiles_of[1 - cur]
                nc.vector.tensor_copy(b[:, 0:hop], a[:, 0:hop])
                step_done(tt(b[:, hop:], a[:, hop:], a[:, 0:E - hop], ALU.add))
                cur = 1 - cur
            end_ = tiles_of[cur]
            step_done(tt(base[:, :], end_[:, :], base[:, :], ALU.subtract))
            step_done(nc.vector.tensor_scalar(base[:, :], base[:, :], float(P), None, ALU.mult))
            ranks = ps_s[:, 0:TT * E].rearrange("p (t e) -> p t e", e=E)
            step_done(tt(pos[:, :, :], ranks, run[src][:, :, :], ALU.add))
            step_done(tt(pos[:, :, :], pos[:, :, :], base[:, None, :].to_broadcast([P, TT, E]), ALU.add))
            step_done(tt(pos[:, :, :], pos[:, :, :], counts, ALU.subtract))
            for k in range(2):
                step_done(tt(posx[:, :, :], pos[:, :, :], pick[k][:, :, :], ALU.mult))
                step_done(tred(slot_f[k][:, :], posx[:, :, :], AX_X, ALU.add))
                ins = nc.vector.tensor_copy(slot[k][:, :], slot_f[k][:, :])
            ins.then_inc(s_slots, 1)
            step_done(tt(past[:, :, :], end_[:, None, :].to_broadcast([P, MAX_TILES, E]),
                         tile_no[:, :, None].to_broadcast([P, MAX_TILES, E]), ALU.is_le))
            step_done(tred(expert[:, :], past[:, :, :], AX_X, ALU.add))
            step_done(nc.vector.tensor_scalar(expert[:, :], expert[:, :], float(E - 1), None, ALU.min))
            step_done(nc.vector.tensor_scalar(need[:, :], expert[:, :], 48.0, 48.0, ALU.mult, ALU.add))
            step_done(nc.vector.tensor_scalar(upper[:, :], expert[:, :], float(SLOTS), float(-SLOTS),
                                              ALU.is_ge, ALU.mult))
            step_done(tt(place[:, :], expert[:, :], upper[:, :], ALU.add))
            nc.vector.tensor_scalar(free_at[:, :], end_[:, :], 1.0, None, ALU.add).then_inc(s_yd, 1)
            dve.wait_ge(s_yd, 1)
            nc.vector.tensor_copy(end[:, :], end_[:, :]).then_inc(s_tab, 1)

            def expert_step(i, par):
                if tile_exists(i, 0):
                    for c in range(2):
                        dve.wait_ge(s_si[c], i + 1)
                        dve.wait_ge(s_h[c], i + 1)
                        if at_least(i, 1):
                            dve.wait_ge(s_ht, i)
                        nc.vector.tensor_tensor(hid[:, c * HB:(c + 1) * HB], act_h[:, c * HB:(c + 1) * HB],
                                                sc_all[:, 2 * c + 1, 0:HB], ALU.mult).then_inc(s_hm[c], 1)
                if tile_exists(i, -1):
                    dve.wait_ge(s_yd, i + 1)
                    if at_least(i, 3):
                        count = 16 * ((i - 1) // 2) if isinstance(i, int) else 8 * (i - 1) if par else 8 * (i - 2)
                        dve.wait_ge(s_yst[1 - par], count)
                    nc.vector.tensor_copy(y_rows[1 - par][:, :], ps_x[:, 0:HID]).then_inc(s_yr, 1)
                if tile_exists(i, 0):
                    dve.wait_ge(s_ht, i + 1)
                    if at_least(i, 2):
                        dve.wait_ge(s_yd, i)
                    nc.vector.tensor_copy(hidT[par][:, 4, :], ps_o[:, 0:P])
                    nc.vector.tensor_copy(hidT[par][0:ITAIL, 5, :], ps_o[0:ITAIL, P:2 * P]).then_inc(s_hT[1], 1)

            expert_steps(dve.Fori, expert_step)

            for t in range(TT):
                dve.wait_ge(s_ga[t % 2], 32 * (t // 2 + 1))
                nc.vector.scalar_tensor_tensor(out=acc[:, t, :], in0=ya[0][t % 2][:, :], scalar=w_top[0][:, t:t + 1],
                                               in1=x2[:, t, :], op0=ALU.mult, op1=ALU.add).then_inc(s_c1, 1)
                dve.wait_ge(s_c1, t + 1)
                nc.vector.scalar_tensor_tensor(out=acc[:, t, :], in0=ya[1][t % 2][:, :], scalar=w_top[1][:, t:t + 1],
                                               in1=acc[:, t, :], op0=ALU.mult, op1=ALU.add).then_inc(s_c2, 1)
                dve.wait_ge(s_c2, t + 1)
                nc.vector.bn_stats(st3[:, t, :], acc[:, t, :]).then_inc(s_c3, 1)
                dve.wait_ge(s_c3, t + 1)
                nc.vector.bn_aggr(mv3[:, t, :], st3[:, t, :]).then_inc(s_c4, 1)
                if t % (TT // 2) == TT // 2 - 1:
                    dve.wait_ge(s_r3, t // (TT // 2) + 1)
                    for u in range(t - TT // 2 + 1, t + 1):
                        nc.vector.tensor_scalar(acc[:, u, :], acc[:, u, :], mv3[:, u, 0:1], rs3[:, u:u + 1],
                                                ALU.subtract, ALU.mult).then_inc(s_x3, 1)

        @block.tensor
        def _(pe):
            mm = nc.tensor.matmul

            def halves(wh, wl, xh_, xl_):
                return [(wl, xh_), (wh, xl_), (wh, xh_)]

            def project(bank, a, which, c, done):
                toks = slice(c * HALF, (c + 1) * HALF)
                passes = [(w, x, k) for w, x in ((wa_l[a], xh), (wa_h[a], xl), (wa_h[a], xh)) for k in range(KT)]
                for i, (w, x, k) in enumerate(passes):
                    ins = mm(bank[:, :], w[:, k, which, :], x[:, k, toks],
                             start=(i == 0), stop=(i == len(passes) - 1))
                ins.then_inc(done, 1)

            def values(n_v, c, part):
                if not isinstance(n_v, int) or n_v > 0:
                    pe.wait_ge(s_v, n_v)
                passes = [(x, w, k) for x, w in ((xh, wv_l), (xl, wv_h), (xh, wv_h)) for k in range(KT)]
                for j in range(2):
                    t0 = c * HALF + (2 * part + j) * P
                    for i, (x, w, k) in enumerate(passes):
                        ins = mm(ps_v[:, 2 * j * D:2 * (j + 1) * D], x[:, k, t0:t0 + P], w[:, k, :],
                                 start=(i == 0), stop=(i == len(passes) - 1))
                ins.then_inc(s_pv, 1)

            def scores(m, par):
                pe.wait_ge(s_q, m + 1)
                pe.wait_ge(s_k, m + 1)
                if not isinstance(m, int) or m > 0:
                    pe.wait_ge(s_p, m)
                for j in range(TH):
                    t = slice(j * P, (j + 1) * P)
                    ins = mm(ps_s[:, t], kT[par][:, t], qT[par][:, t], start=True, stop=True)
                ins.then_inc(s_s, 1)

            def attend(m, s, it_of):
                a, c = s // 2, s % 2
                pe.wait_ge(s_p, m + 1)
                pe.wait_ge(s_v, 4 * it_of + 2 * c + 2)
                if not isinstance(m, int) or m > 0:
                    pe.wait_ge(s_sq, m)
                for j in range(TH):
                    t = slice(j * P, (j + 1) * P)
                    ins = mm(ps_o[:, t], v_sb[c][:, j, a, :], pT[s % 2][:, t], start=True, stop=True)
                ins.then_inc(s_o, 1)

            def out_product(i, c):
                pe.wait_ge(s_go, 4 * i + 3 + c)
                pe.wait_ge(s_wosc, i + 1)
                for b in range(2):
                    if not (isinstance(i, int) and i == 0 and c == 0):
                        pe.wait_ge(s_ya[b], 2 * i + c)
                    for t in range(2):
                        t0 = (TH * c + 2 * b + t) * P
                        for a in range(2):
                            ins = mm(ps_y[b][:, t * HID:(t + 1) * HID], go[a][:, t0:t0 + P], wo_s[:, a, :],
                                     start=(a == 0), stop=(a == 1))
                    ins.then_inc(s_y[b], 1)

            def step(it, s, first):
                n = 4 * it + s
                a, c = s // 2, s % 2
                lag, lag_s, lag_it = n - 1, (s - 1) % 4, (it - 1 if s == 0 else it)
                started = not (first and s == 0)
                if c == 0:
                    pe.wait_ge(s_wasp[a], it + 1)
                if started:
                    pe.wait_ge(s_q, n)
                project(ps_q, a, 0, c, s_pq)
                if s == 0:
                    pe.wait_ge(s_wvsp, it + 1)
                if s < 2:
                    values(4 * it + 2 * s, c, 0)
                if started:
                    scores(lag, 1 - s % 2)
                    pe.wait_ge(s_k, n)
                project(ps_k, a, 1, c, s_pk)
                if s < 2:
                    values(4 * it + 2 * s + 1, c, 1)
                if started:
                    attend(lag, lag_s, lag_it)
                    pe.wait_ge(s_g, n)
                project(ps_g, a, 2, c, s_pg)
                if s < 2 and not first:
                    out_product(it - 1, s)

            pe.wait_ge(s_xs, 1)
            for s in range(4):
                step(0, s, True)
                if s == 0:
                    pe.wait_ge(s_decay, 1)
            with pe.Fori(1, PAIRS) as it:
                for s in range(4):
                    step(it, s, False)
            scores(STEPS - 1, 1)
            out_product(PAIRS - 1, 0)
            attend(STEPS - 1, 3, PAIRS - 1)
            out_product(PAIRS - 1, 1)

            pe.wait_ge(s_sqa, STEPS)
            pe.wait_ge(s_const, 4)
            pe.wait_ge(s_ya[1], 2 * PAIRS)
            for t in range(TT):
                ins = mm(ps_x[:, t:t + 1], sq_acc[:, t * P:(t + 1) * P], ones[:, 0:1], start=True, stop=True)
            ins.then_inc(s_pms, 1)
            pe.wait_ge(s_wl, 48)
            pe.wait_ge(s_ms, 1)
            pe.wait_ge(s_sq, STEPS)
            pe.wait_ge(s_ya[0], 2 * PAIRS)

            def turn(bank, src, done, n=KT):
                for k in range(n):
                    ins = nc.tensor.transpose(bank[:, k * P:(k + 1) * P], src(k), ident[:, :])
                ins.then_inc(done, 1)

            def cross(p, par):
                nxt = 1 - par
                if has(p, 0):
                    pe.wait_ge(s_pe, p + 1)
                    for b in range(2):
                        if at_least(p, 1):
                            pe.wait_ge(s_pT[b], p)
                        turn(ps_pt[b], lambda j: prob[par][:, 8 * b + 2 * j:8 * b + 2 * j + 2, :]
                             .rearrange("p h t -> p (h t)"), s_pt[b], 4)
                if has(p, 1):
                    pe.wait_ge(s_x1, p + 2)
                    if at_least(p, 2):
                        pe.wait_ge(s_lg, p - 1)
                    turn(ps_x1, lambda k: x1[nxt][:, k * P:(k + 1) * P], s_x1t)
                if has(p, 0):
                    for b in range(2):
                        pe.wait_ge(s_pT[b], p + 1)
                    pe.wait_ge(s_vx, p + 1)
                    if at_least(p, 1):
                        pe.wait_ge(s_z2, p)
                    for j in range(XH // 2):
                        f, r = j // NR, j % NR
                        ins = mm(ps_x[:, 64 * j:64 * j + 64], probT[f][:, r, :], vx[par][:, :, 2 * f + r // 2, :],
                                 start=True, stop=True)
                    ins.then_inc(s_pvx, 1)
                if has(p, -1):
                    pe.wait_ge(s_x2, p)
                    if has(p, 1):
                        pe.wait_ge(s_x1T, p + 2)
                    else:
                        pe.wait_ge(s_lg, p - 1)
                    turn(ps_x1, lambda k: x2s[nxt][:, k * P:(k + 1) * P], s_x2t)
                if has(p, 1):
                    pe.wait_ge(s_x1T, p + 2)
                    pe.wait_ge(s_kx, p + 2)
                    if at_least(p, 0):
                        pe.wait_ge(s_sub, 2 * p + 2)
                    for f in range(2):
                        for b in range(2):
                            for r in range(NR):
                                rows = slice(r * ROWS, (r + 1) * ROWS)
                                cols = slice(b * SEQ, (b + 1) * SEQ)
                                ins = mm(ps_sc[r][cols, f * P:(f + 1) * P], x1T[nxt][rows, f, cols],
                                         kx[nxt][rows, b, f, :], start=True, stop=True)
                    ins.then_inc(s_xs_, 1)
                if has(p, 0):
                    pe.wait_ge(s_xo, 2 * p + 2)
                    turn(ps_x, lambda k: xo[:, k * P:(k + 1) * P], s_xot)
                if has(p, -1):
                    pe.wait_ge(s_x2T, p)
                    for k in range(KT):
                        ins = mm(ps_x1[:, 256:256 + E], x2T[:, k, :], wg[:, k, :], start=(k == 0), stop=(k == KT - 1))
                    ins.then_inc(s_rt, 1)
                if has(p, 0):
                    pe.wait_ge(s_xoT, p + 1)
                    for k in range(KT):
                        ins = mm(ps_x[:, 0:HID], xoT[:, k, :], wc[:, k, :], start=(k == 0), stop=(k == KT - 1))
                    ins.then_inc(s_wcd, 1)

            cross_steps(pe.Fori, cross)

            pe.wait_ge(s_both, 1)
            flat = both[:, :, :].rearrange("p t e -> p (t e)")
            mm(ps_s[:, 0:TT * E], before[:, :], flat, start=True, stop=True)
            mm(ps_s[:, TT * E:2 * TT * E], ones[:, :], flat, start=True, stop=True).then_inc(s_route_pe, 1)
            pe.wait_ge(s_tab, 1)

            def expert(i, par):
                nxt = 1 - par
                if tile_exists(i, 0):
                    loads = pe.value_load(one(need, i), min_val=48, max_val=48 * E)
                    at = pe.value_load(one(place, i), min_val=0, max_val=SLOTS - 1)
                    pe.wait_ge(s_tT, i + 1)
                    pe.wait_ge(s_we, loads)
                    for c in range(2):
                        if at_least(i, 1):
                            pe.wait_ge(s_hm[c], i)
                        for g in range(2):
                            for k in range(KT):
                                col = g * INTER + c * HB
                                ins = mm(sc_all[:, 2 * c + g, 0:HB], xtT[par][:, k, :],
                                         w13[:, bass.ds(at, 1), k, col:col + HB].rearrange("p a n -> p (a n)"),
                                         start=(k == 0), stop=(k == KT - 1))
                        ins.then_inc(s_h[c], 1)
                if tile_exists(i, 1):
                    pe.wait_ge(s_xt[nxt], (16 * ((i + 1) // 2 + 1)) if isinstance(i, int)
                               else 8 * (i + 3) if par else 8 * (i + 2))
                    if at_least(i, 0):
                        pe.wait_ge(s_tT, i + 1)
                    turn(ps_x1, lambda k: xt_rows[nxt][:, k * P:(k + 1) * P], s_tt)
                if tile_exists(i, -1):
                    at1 = pe.value_load(one(place, i - 1), min_val=0, max_val=SLOTS - 1)
                    for b in range(2):
                        pe.wait_ge(s_hT[b], i)
                    if at_least(i, 2):
                        pe.wait_ge(s_yr, i - 1)
                    for k in range(ITILES):
                        rows = P if k < ITILES - 1 else ITAIL
                        ins = mm(ps_x[:, 0:HID], hidT[nxt][0:rows, k, :],
                                 w2[0:rows, bass.ds(at1, 1), k, :].rearrange("p a n -> p (a n)"),
                                 start=(k == 0), stop=(k == ITILES - 1))
                    ins.then_inc(s_yd, 1)
                if tile_exists(i, 0):
                    for c in range(2):
                        pe.wait_ge(s_hm[c], i + 1)
                    if at_least(i, 1):
                        for b in range(2):
                            pe.wait_ge(s_hT[b], i)
                    for k in range(ITILES):
                        rows = P if k < ITILES - 1 else ITAIL
                        bank, col = (ps_s, k) if k < 4 else (ps_o, k - 4)
                        ins = nc.tensor.transpose(bank[0:rows, col * P:(col + 1) * P], hid[:, k * P:k * P + rows],
                                                  ident[:, :])
                    ins.then_inc(s_ht, 1)

            expert_steps(pe.Fori, expert)


def kernel(**inputs):
    import numpy as np
    import concourse.bacc as bacc
    from concourse.bass_utils import run_bass_kernel_spmd

    f = {k: np.ascontiguousarray(v) for k, v in inputs.items()}
    x = f["x"].reshape(T, HID)
    wqkv = f["L0_attn_w_qkv"].reshape(KT, P, 3, H, D)
    wgate = f["L0_attn_w_gate"].reshape(KT, P, 1, H, D)
    wqkg = np.concatenate([wqkv[:, :, 0:2], wgate], axis=2)
    arrays = {
        "xT": x.T,
        "x": x,
        "wa": wqkg.transpose(3, 1, 0, 2, 4),
        "wv": wqkv[:, :, 2].reshape(KT, P, PAIRS, 2, D).transpose(2, 1, 0, 3, 4),
        "wo": f["L0_attn_w_out"].reshape(PAIRS, 2, D, HID).transpose(0, 2, 1, 3),
        "ctx": f["ctx_512"].reshape(T, CTX),
        "ctxT": f["ctx_512"].reshape(T, CTX).T,
        "wcT": f["L0_xattn_Wc"].T,
        "bc": f["L0_xattn_bc"].reshape(1, HID),
        "wgT": f["L0_ffn_Wg"].T,
        "w13": np.stack([f["L0_ffn_w1"], f["L0_ffn_w3"]], 1).reshape(E, 2 * INTER, KT, P).transpose(0, 3, 2, 1),
        "w2a": f["L0_ffn_w2"].transpose(0, 2, 1)[:, :(ITILES - 1) * P].reshape(E, ITILES - 1, P, HID)
        .transpose(0, 2, 1, 3),
        "w2b": f["L0_ffn_w2"].transpose(0, 2, 1)[:, (ITILES - 1) * P:],
        "rms": f["L0_attn_rms_weight"].reshape(H, D).T,
        "slope": f["L0_attn_slope_rate"].reshape(1, H),
    }
    nc = bacc.Bacc("TRN2", target_bir_lowering=False, num_devices=1)
    d, sent = {}, {}
    for name, a in arrays.items():
        a = np.ascontiguousarray(a)
        sent[f"in_{name}"] = a
        d[name] = nc.dram_tensor(f"in_{name}", a.shape, mybir.dt.from_np(a.dtype), kind="ExternalInput").ap()
    d["out"] = nc.dram_tensor("out_x", (T, HID), F32, kind="ExternalOutput").ap()
    decoder_layer(nc, d)
    got = run_bass_kernel_spmd(nc, [sent], core_ids=[0])
    return got.results[0]["out_x"].reshape(BATCHES, SEQ, HID)
```

```python
from contextlib import ExitStack

import concourse.bass as bass
import concourse.mybir as mybir
from concourse.alu_op_type import AluOpType as ALU

ACT = mybir.ActivationFunctionType
F32 = mybir.dt.float32
F32R = mybir.dt.float32r
I32 = mybir.dt.int32
U32 = mybir.dt.uint32
AX_X = mybir.AxisListType.X

P = 128
BATCHES, SEQ, HID = 16, 64, 256
T = BATCHES * SEQ
KT = HID // P
TT = T // P
H, D = 16, 128
HALF = 512
TH = HALF // P
PAIRS = H // 2
STEPS = 2 * H
GROUPS, HD = 4, 16
XH = GROUPS * 4
CTX = GROUPS * HD
ROWS = 32
NR = P // ROWS
E, INTER = 8, 704
ITILES = -(-INTER // P)
HB = INTER // 2
ITAIL = INTER - (ITILES - 1) * P
SLOTS = 4
MIN_TILES = 2 * T // P
MAX_TILES = MIN_TILES + E - 1
TABLE = MAX_TILES + 2
EPS_RMS = 1e-6
EPS_LN = 1e-5


def decoder_layer(nc, d):
    with ExitStack() as ctx:
        def sb(name, shape, dt=F32):
            return ctx.enter_context(nc.sbuf_tensor(name, shape, dt))

        def psum(name):
            return ctx.enter_context(nc.psum_tensor(name, [P, 512], F32))

        def sem(name):
            return ctx.enter_context(nc.semaphore(name))

        acc = sb("acc", [P, TT, HID])
        rms_w = sb("rms_w", [P, H])
        slope = sb("slope", [P, H])
        ident = sb("ident", [P, P])
        ones = sb("ones", [P, P])
        before = sb("before", [P, P])
        mhalf = sb("mhalf", [P, TT])
        eps_ln = sb("eps_ln", [P, 1])
        x_rows = sb("x_rows", [P, TT, HID])
        x2 = sb("x2", [P, TT, HID])
        k_all = sb("k_all", [P, BATCHES, 2, P])
        v_all = sb("v_all", [P, BATCHES, GROUPS, 2 * HD])
        wc = sb("wc", [P, KT, HID])
        wg = sb("wg", [P, KT, E])
        bc = sb("bc", [P, HID])
        st1 = sb("st1", [P, TT, 6])
        mv1 = sb("mv1", [P, TT, 2])
        rs1 = sb("rs1", [P, TT])
        z2 = [sb(f"z2_{i}", [P, HID]) for i in range(2)]
        st2 = sb("st2", [P, TT, 6])
        mv2 = sb("mv2", [P, TT, 2])
        rs2 = sb("rs2", [P, TT])
        x1T = [sb(f"x1T_{i}", [P, KT, P]) for i in range(2)]
        prob = [sb(f"prob{i}", [P, XH, SEQ]) for i in range(2)]
        pmax = sb("pmax", [P, XH])
        prob_sum = [sb(f"prob_sum{i}", [P, XH]) for i in range(2)]
        prec = sb("prec", [P, XH])
        probT = [sb(f"probT{i}", [P, 4, P]) for i in range(2)]
        xo = sb("xo", [P, HID])
        xoT = sb("xoT", [P, KT, P])
        x2T = sb("x2T", [P, KT, P])
        ms = sb("ms", [P, TT])
        zero = sb("zero", [P, HID])
        numbers = sb("numbers", [P, TABLE])
        base = sb("base", [P, E])
        logit = sb("logit", [P, TT, E])
        best = sb("best", [P, TT, E])
        best_at = sb("best_at", [P, TT, E], U32)
        chosen = sb("chosen", [P, TT, 2])
        pick = sb("pick", [P, TT, 2, E])
        both = sb("both", [P, TT, E])
        sofar = sb("sofar", [P, TT + 1, E])
        pos = sb("pos", [P, TT, E])
        pos_of = sb("pos_of", [P, TT, 2, E])
        slot_of = sb("slot_of", [P, TT, 2], U32)
        slot = [sb(f"slot{i}", [P, TT], U32) for i in range(2)]
        lower = sb("lower", [P, TT])
        upper = sb("upper", [P, TT])
        ratio = sb("ratio", [P, TT])
        w_best = [sb(f"w_best{i}", [P, TT]) for i in range(2)]
        w_part = sb("w_part", [P, 4, TT])
        weight = [sb(f"weight{i}", [P, TT]) for i in range(2)]
        counts = sb("counts", [P, E])
        more = sb("more", [P, E, TT])
        tiles_of = sb("tiles_of", [P, E])
        run = [sb(f"run{i}", [P, E]) for i in range(2)]
        past = sb("past", [P, TABLE, E - 1])
        skip = sb("skip", [P, E - 1])
        skips = sb("skips", [P, TABLE, E - 1])
        row_f = sb("row_f", [P, TABLE])
        expert = sb("expert", [P, TABLE])
        wrap = sb("wrap", [P, TABLE])
        halves_of = sb("halves_of", [P, 2, MIN_TILES])
        pairs_f = sb("pairs_f", [P, 2])
        parity_f = sb("parity_f", [P, 1])
        row = sb("row", [P, TABLE], I32)
        place = sb("place", [P, TABLE], I32)
        need = sb("need", [P, TABLE], I32)
        which = sb("which", [P, TABLE], I32)
        free_at = sb("free_at", [P, E], I32)
        seen = sb("seen", [P, 3])
        steps = sb("steps", [P, 2], I32)
        stores_lo = sb("stores_lo", [P, 2], I32)
        stores_all = sb("stores_all", [P, 2], I32)
        x_sorted = nc.dram_tensor("x_sorted", (E * T, HID), F32, kind="Internal").ap()
        y_sorted = nc.dram_tensor("y_sorted", (E * T, HID), F32, kind="Internal").ap()
        rms_r = sb("rms_r", [P, TT])

        region = ExitStack()

        def early(name, shape, dt=F32):
            return region.enter_context(nc.sbuf_tensor(name, shape, dt))

        ctx_rows = early("ctx_rows", [P, BATCHES, CTX])
        x_raw = early("x_raw", [P, KT, T])
        xh = early("xh", [P, KT, T], F32R)
        xl = early("xl", [P, KT, T], F32R)
        wa_raw = [early(f"w{a}_raw", [P, KT, 3, D]) for a in range(2)]
        wv_raw = early("wv_raw", [P, KT, 2, D])
        wo_raw = early("wo_raw", [P, 2, HID])
        wa_h = [early(f"w{a}_h", [P, KT, 3, D], F32R) for a in range(2)]
        wa_l = [early(f"w{a}_l", [P, KT, 3, D], F32R) for a in range(2)]
        wv_h = early("wv_h", [P, KT, 2 * D], F32R)
        wv_l = early("wv_l", [P, KT, 2 * D], F32R)
        wo_s = early("wo_s", [P, 2, HID])
        wo_h = early("wo_h", [P, 2, HID], F32R)
        wo_l = early("wo_l", [P, 2, HID], F32R)
        dist = early("dist", [P, P])
        visible = early("visible", [P, P])
        decay = early("decay", [P, H, P])
        qT = [early(f"qT{i}", [P, HALF]) for i in range(2)]
        kT = [early(f"kT{i}", [P, HALF]) for i in range(2)]
        tg = [early(f"tg{i}", [P, HALF]) for i in range(2)]
        pT = [early(f"pT{i}", [P, HALF]) for i in range(2)]
        v_sb = [early(f"v{c}", [P, TH, 2, D]) for c in range(2)]
        go = [early(f"go{i}", [P, HALF]) for i in range(2)]
        go_h = [early(f"go{a}_h", [P, T], F32R) for a in range(2)]
        go_l = [early(f"go{a}_l", [P, T], F32R) for a in range(2)]
        o_sq = [early(f"o_sq{i}", [P, HALF]) for i in range(2)]
        sq_acc = early("sq_acc", [P, T])

        region.close()
        xt_rows = [sb(f"xt_rows{i}", [P, HID]) for i in range(2)]
        xtT = [sb(f"xtT{i}", [P, KT, P]) for i in range(2)]
        act_h = sb("act_h", [P, INTER])
        hid = sb("hid", [P, INTER])
        hidT = [sb(f"hidT{i}", [P, ITILES, P]) for i in range(2)]
        y_rows = [sb(f"y_rows{i}", [P, HID]) for i in range(2)]
        y_got = [x_rows, sb("y_got1", [P, TT, HID])]
        st3 = sb("st3", [P, TT, 6])
        mv3 = sb("mv3", [P, TT, 2])
        rs3 = sb("rs3", [P, TT])
        w13 = sb("w13", [P, SLOTS, KT, 2 * INTER])
        w2 = sb("w2", [P, E, ITILES, HID])

        sc_all = ctx.enter_context(nc.psum_tensor("ps_qkgv", [P, NR, 512], F32))
        ps_q, ps_k, ps_g, ps_v = (sc_all[:, r, :] for r in range(NR))
        ps_s, ps_o, ps_y0, ps_y1 = (psum(n) for n in ("ps_s", "ps_o", "ps_y0", "ps_y1"))
        ps_y = [ps_y0, ps_y1]

        s_x = [sem(f"x{c}_loaded") for c in range(2)]
        s_slope = sem("slope_loaded")
        s_small = sem("small_loaded")
        s_wa = [sem(f"w{a}_loaded") for a in range(2)]
        s_wv = sem("wv_loaded")
        s_wo = sem("wo_loaded")
        s_xs = [sem(f"x{c}_split") for c in range(2)]
        s_dist = sem("dist_made")
        s_vis = sem("visible_made")
        s_arg_pre = sem("slope_negated")
        s_arg = sem("decay_arg")
        s_exp = sem("decay_exp")
        s_decay = sem("decay_made")
        s_zero = sem("sums_zeroed")
        s_hi = sem("hi_made")
        s_wasp = [sem(f"w{a}_split") for a in range(2)]
        s_wvsp = sem("wv_split")
        s_wosp = sem("wo_split")
        s_pq, s_pk, s_pg, s_pv = sem("q_projected"), sem("k_projected"), sem("g_projected"), sem("v_projected")
        s_q, s_k, s_g, s_v = sem("q_ready"), sem("k_ready"), sem("g_ready"), sem("v_ready")
        s_s, s_p, s_o, s_go, s_sq = sem("scores_done"), sem("p_ready"), sem("o_done"), sem("go_ready"), sem("o_squared")
        s_sqa = sem("squares_added")
        s_gh, s_gl = sem("go_high_made"), sem("go_split")
        s_wos, s_woh = sem("wo_scaled"), sem("wo_high_made")
        s_y = [sem(f"y{i}_done") for i in range(2)]
        s_ya = [sem(f"y{i}_added") for i in range(2)]
        s_out = sem("out_stored")
        s_const, s_cm = sem("constants_made"), sem("constants_filled")
        s_zt, s_xz, s_rc = sem("zero_tile"), sem("x_sorted_zeroed"), sem("routing_constants")
        s_xr = sem("x_rows_loaded")
        s_kz, s_vz = sem("k_zeroed"), sem("v_zeroed")
        s_kl, s_cl, s_wl = sem("k_loaded"), sem("ctx_loaded"), sem("cross_weights_loaded")
        s_va = sem("v_arranged")
        s_pms, s_ms, s_rms = sem("squares_summed"), sem("mean_square"), sem("rms_ready")
        s_z1, s_b1, s_m1, s_e1, s_r1 = sem("z1"), sem("bn1"), sem("mv1"), sem("eps1"), sem("rstd1")
        s_x1, s_x1b = sem("x1_ready"), sem("x1_plus_bias")
        s_z2, s_b2, s_m2, s_e2, s_r2 = sem("z2"), sem("bn2"), sem("mv2"), sem("eps2"), sem("rstd2")
        s_x2 = sem("x2_ready")
        s_x1t, s_x1T = sem("x1_turned"), sem("x1T_ready")
        s_sc, s_mx, s_sub, s_pe = sem("cross_scores"), sem("row_max"), sem("max_off"), sem("exp_done")
        s_pr = sem("sum_inverse")
        s_pt, s_pT = [sem(f"prob_turned{i}") for i in range(2)], [sem(f"probT_ready{i}") for i in range(2)]
        s_pvx, s_xo = sem("cross_values"), sem("xo_ready")
        s_xot, s_xoT, s_wcd = sem("xo_turned"), sem("xoT_ready"), sem("wc_done")
        s_x2t, s_x2T, s_rt, s_lg = sem("x2_turned"), sem("x2T_ready"), sem("router_done"), sem("logits_ready")
        s_sort, s_at, s_ch, s_pk2 = sem("logits_sorted"), sem("places_found"), sem("choice_numbers"), sem("choice_made")
        s_both, s_cnt, s_pos, s_po2 = sem("choices_added"), sem("rows_counted"), sem("position_ready"), sem("slots_found")
        s_slots, s_scat, s_ordered = sem("slots_ready"), sem("rows_scattered"), sem("slots_ordered")
        s_tot, s_r, s_w = sem("totals_counted"), sem("table_step"), sem("weight_step")
        s_dif, s_rexp = sem("logit_difference"), sem("ratio_ready")
        s_seen = sem("stores_seen")
        s_row, s_tab = sem("row_table"), sem("tile_tables")
        s_w13, s_w2 = sem("w13_loaded"), sem("w2_loaded")
        s_xt = [sem(f"tile_loaded{i}") for i in range(2)]
        s_tt, s_tT = sem("tile_turned"), sem("tileT_ready")
        s_h = [sem("hidden_done0"), sem("one_and_hidden_done1")]
        s_si = [sem(f"silu_done{i}") for i in range(2)]
        s_hm = [sem(f"hidden_ready{i}") for i in range(2)]
        s_ht, s_hT = sem("hidden_turned"), [sem(f"hiddenT_ready{i}") for i in range(2)]
        s_yd, s_yr = sem("outputs_done"), sem("y_copied")
        s_yst = [sem(f"y_stored{i}") for i in range(2)]
        s_ga = [[sem(f"gathered{k}_{t}") for t in range(TT)] for k in range(2)]
        s_c1, s_c2, s_c3, s_c4 = sem("added_first"), sem("added_second"), sem("bn3"), sem("mv3")
        s_e3, s_r3, s_x3 = sem("eps3"), sem("rstd3"), sem("x3_ready")

        ps_sc = [sc_all[:, r, :] for r in range(NR)]
        ps_pt = [ps_s, ps_o]
        ps_x1, ps_x = ps_y0, ps_y1

        block = ctx.enter_context(nc.Block())

        CROSS_STEPS = range(-4, TT + 2)

        def has(p):
            return 0 <= p < TT

        def expert_steps(eng, stage):
            last = eng.value_load(steps[0:1, 0:1], min_val=MIN_TILES - 6, max_val=MAX_TILES - 5) + 3
            even = eng.value_load(steps[0:1, 1:2], min_val=0, max_val=1)
            stage(-1, 1, False, True, False)
            stage(0, 0, True, True, False)
            stage(1, 1, True, True, True)
            stage(2, 0, True, True, True)
            with eng.Fori(3, last, 2) as i:
                stage(i, 1, True, True, True)
                stage(i + 1, 0, True, True, True)
            stage(last, 1, True, True, True)
            with eng.If(even > 0):
                stage(last + 1, 0, True, True, True)
                stage(last + 2, 1, True, False, True)
                stage(last + 3, 0, False, False, True)
            with eng.Else():
                stage(last + 1, 0, True, False, True)
                stage(last + 2, 1, False, False, True)

        def later(i, n):
            return i >= n if isinstance(i, int) else n <= 3

        def one(t, i):
            return t[0:1, i:i + 1] if isinstance(i, int) else t[0:1, bass.ds(i, 1)]

        @block.sync
        def _(sp):
            def load_pair(i, first):
                if not first:
                    sp.wait_ge(s_wasp[0], i)
                sp.dma_start(wa_raw[0][:, :, :, :], d["wa"][2 * i]).then_inc(s_wa[0], 16)
                if not first:
                    sp.wait_ge(s_wvsp, i)
                sp.dma_start(wv_raw[:, :, :, :], d["wv"][i]).then_inc(s_wv, 16)
                if not first:
                    sp.wait_ge(s_wosp, i)
                sp.dma_start(wo_raw[:, :, :], d["wo"][i]).then_inc(s_wo, 16)
                if not first:
                    sp.wait_ge(s_wasp[1], i)
                sp.dma_start(wa_raw[1][:, :, :, :], d["wa"][2 * i + 1]).then_inc(s_wa[1], 16)

            sp.dma_start(slope[:, :], d["slope"].to_broadcast([P, H])).then_inc(s_slope, 16)
            for c in range(2):
                sp.dma_start(x_raw[:, :, c * HALF:(c + 1) * HALF],
                             d["xT"].rearrange("(k p) t -> p k t", p=P)[:, :, c * HALF:(c + 1) * HALF]
                             ).then_inc(s_x[c], 16)
                if c == 0:
                    load_pair(0, True)
            sp.dma_start(rms_w[:, :], d["rms"]).then_inc(s_small, 16)
            for hh in range(2):
                sp.dma_start(ctx_rows[hh * SEQ:(hh + 1) * SEQ, :, :],
                             d["ctx"].rearrange("(b t) d -> t b d", t=SEQ)).then_inc(s_cl, 16)
            with sp.Fori(1, PAIRS) as i:
                load_pair(i, False)
            sp.dma_start(x_rows[:, :, :], d["x"].rearrange("(t p) n -> p t n", p=P)).then_inc(s_xr, 16)
            sp.wait_ge(s_kz, 1)
            for r in range(NR):
                for hh in range(2):
                    for f in range(2):
                        p0, g = r * ROWS + hh * HD, 2 * f + r // 2
                        sp.dma_start(k_all[p0:p0 + HD, :, f, hh * SEQ:(hh + 1) * SEQ],
                                     d["ctxT"][g * HD:(g + 1) * HD, :].rearrange("d (b t) -> d b t", t=SEQ)
                                     ).then_inc(s_kl, 16)
            sp.dma_start(wc[:, :, :], d["wcT"].rearrange("(k p) n -> p k n", p=P)).then_inc(s_wl, 16)
            sp.dma_start(wg[:, :, :], d["wgT"].rearrange("(k p) n -> p k n", p=P)).then_inc(s_wl, 16)
            sp.dma_start(bc[:, :], d["bc"].to_broadcast([P, HID])).then_inc(s_wl, 16)
            sp.wait_ge(s_zt, 1)
            for rows in (x_sorted, y_sorted):
                sp.dma_start(rows.rearrange("(p t) n -> p t n", p=P),
                             zero[:, None, :].to_broadcast([P, E * TT, HID])).then_inc(s_xz, 16)

            def load_w13(e):
                sp.dma_start(w13[:, e % SLOTS, :, :], d["w13"][e]).then_inc(s_w13, 16)
                sp.wait_ge(s_w13, 16 * (e + 1))

            def load_w2(e):
                sp.dma_start(w2[:, e, 0:ITILES - 1, :], d["w2a"][e]).then_inc(s_w2, 16)
                sp.dma_start(w2[0:ITAIL, e, ITILES - 1, :], d["w2b"][e]).then_inc(s_w2, 16)

            sp.wait_ge(s_pms, 1)
            for b in range(2):
                sp.wait_ge(s_y[b], 2 * PAIRS)
            for e in range(E):
                if e < SLOTS:
                    load_w13(e)
                load_w2(e)
                sp.wait_ge(s_w2, 32 * (e + 1))
            sp.wait_ge(s_tab, 1)
            for e in range(SLOTS, E):
                free = sp.value_load(free_at[0:1, e - SLOTS:e - SLOTS + 1], min_val=1, max_val=MAX_TILES + 1)
                sp.wait_ge(s_h[1], free)
                load_w13(e)
            for t0, t1 in ((0, TT // 2), (TT // 2, TT - 2), (TT - 2, TT)):
                sp.wait_ge(s_x3, t1)
                sp.dma_start(d["out"].rearrange("(t p) n -> p t n", p=P)[:, t0:t1, :],
                             acc[:, t0:t1, :]).then_inc(s_out, 16)
            sp.wait_ge(s_out, 48)

        @block.scalar
        def _(act):
            act.wait_ge(s_arg, 1)
            nc.scalar.activation(decay[:, :, :], decay[:, :, :], ACT.Exp).then_inc(s_exp, 1)

            def values(n_v, c, part, wait_free, it):
                act.wait_ge(s_pv, n_v + 1)
                if wait_free:
                    act.wait_ge(s_o, 4 * it - 1 + c)
                nc.scalar.activation(v_sb[c][:, 2 * part:2 * part + 2, :, :],
                                     ps_v[:, :].rearrange("p (j a e) -> p j a e", j=2, a=2),
                                     ACT.Silu).then_inc(s_v, 1)

            def high(s):
                a, c = s // 2, s % 2
                nc.scalar.activation(go_h[a][:, c * HALF:(c + 1) * HALF], go[s % 2][:, :], ACT.Copy).then_inc(s_gh, 1)

            def step(it, s, first):
                n = 4 * it + s
                par = s % 2
                act.wait_ge(s_pq, n + 1)
                if not (first and s < 2):
                    act.wait_ge(s_s, n - 1)
                nc.scalar.activation(qT[par][:, :], ps_q[:, :], ACT.Silu).then_inc(s_q, 1)
                if s < 2:
                    values(4 * it + 2 * s, s, 0, not first, it)
                act.wait_ge(s_pk, n + 1)
                nc.scalar.activation(kT[par][:, :], ps_k[:, :], ACT.Silu).then_inc(s_k, 1)
                if s < 2:
                    values(4 * it + 2 * s + 1, s, 1, False, it)
                if not (first and s == 0):
                    act.wait_ge(s_go, n)
                    if not (first and s < 3):
                        act.wait_ge(s_sqa, n - 2)
                    nc.scalar.activation(o_sq[1 - par][:, :], ps_o[:, :], ACT.Square).then_inc(s_sq, 1)
                    high((s - 1) % 4)
                act.wait_ge(s_pg, n + 1)
                nc.scalar.activation(tg[par][:, :], ps_g[:, :], ACT.Tanh, scale=0.5).then_inc(s_g, 1)

            for s in range(4):
                step(0, s, True)
            act.wait_ge(s_vz, 1)
            act.wait_ge(s_cl, 32)
            for hh in range(2):
                rows = slice(hh * SEQ, (hh + 1) * SEQ)
                nc.scalar.activation(v_all[rows, :, :, hh * HD:(hh + 1) * HD],
                                     ctx_rows[rows, :, :].rearrange("p b (g d) -> p b g d", g=GROUPS),
                                     ACT.Copy).then_inc(s_va, 1)
            with act.Fori(1, PAIRS) as it:
                for s in range(4):
                    step(it, s, False)
            act.wait_ge(s_go, STEPS)
            act.wait_ge(s_sqa, STEPS - 2)
            nc.scalar.activation(o_sq[(STEPS - 1) % 2][:, :], ps_o[:, :], ACT.Square).then_inc(s_sq, 1)
            high(3)

            def exponentials(q, f):
                act.wait_ge(s_sub, 2 * q + f + 1)
                if f == 0 and q >= 2:
                    act.wait_ge(s_pr, q - 1)
                for h in range(f * XH // 2, (f + 1) * XH // 2):
                    ins = nc.scalar.activation(prob[q % 2][:, h, :], prob[q % 2][:, h, :], ACT.Exp,
                                               accum_out=prob_sum[q % 2][:, h:h + 1])
                if f == 1:
                    ins.then_inc(s_pe, 1)

            for p in CROSS_STEPS:
                if has(p + 3):
                    act.wait_ge(s_x1t, p + 4)
                    if p + 2 >= 1:
                        act.wait_ge(s_sc, p + 2)
                    nc.scalar.activation(x1T[(p + 3) % 2][:, :, :].rearrange("p k t -> p (k t)"),
                                         ps_o[:, 0:HID], ACT.Copy, scale=HD ** -0.5).then_inc(s_x1T, 1)
                if has(p - 1):
                    act.wait_ge(s_x2t, p)
                    if p >= 2:
                        act.wait_ge(s_rt, p - 1)
                    nc.scalar.activation(x2T[:, :, :].rearrange("p k t -> p (k t)"),
                                         ps_s[:, 0:HID], ACT.Copy).then_inc(s_x2T, 1)
                if has(p):
                    act.wait_ge(s_xot, p + 1)
                    if p >= 1:
                        act.wait_ge(s_wcd, p)
                    nc.scalar.activation(xoT[:, :, :].rearrange("p k t -> p (k t)"),
                                         ps_x[:, 0:HID], ACT.Copy).then_inc(s_xoT, 1)
                if has(p + 2):
                    exponentials(p + 2, 0)
                if has(p + 1):
                    for b in range(2):
                        act.wait_ge(s_pt[b], p + 2)
                        if p >= 0:
                            act.wait_ge(s_pvx, p + 1)
                        nc.scalar.activation(probT[b][:, :, :].rearrange("p j t -> p (j t)"),
                                             ps_pt[b][:, :], ACT.Copy).then_inc(s_pT[b], 1)
                if has(p + 2):
                    exponentials(p + 2, 1)
            act.wait_ge(s_row, 1)

            def load_tile(r, par):
                act.dma_start(xt_rows[par][:, :], x_sorted[bass.ds(r, P), :]).then_inc(s_xt[par], 16)

            def row_at(i):
                return act.value_load(one(row, i), min_val=0, max_val=E * T - P)

            first_rows = [row_at(i) for i in range(2)]
            act.wait_ge(s_scat, 2 * TT * 16)
            for i in range(2):
                load_tile(first_rows[i], i)
            act.wait_ge(s_dif, 1)
            nc.scalar.activation(ratio[:, :], ratio[:, :], ACT.Exp).then_inc(s_rexp, 1)

            def expert_stage(i, par, h, t, y):
                nxt = 1 - par
                if h and t:
                    r = row_at(i + 2)
                if y:
                    r_y = row_at(i - 1)
                if h and t:
                    act.wait_ge(s_tt, i + 1)
                    load_tile(r, par)
                if h:
                    for c in range(2):
                        act.wait_ge(s_h[c], i + 1 + c)
                        if later(i, 1):
                            act.wait_ge(s_hm[c], i)
                        nc.scalar.activation(act_h[:, c * HB:(c + 1) * HB], sc_all[:, 2 * c, 0:HB], ACT.Silu
                                             ).then_inc(s_si[c], 1)
                if t:
                    act.wait_ge(s_tt, i + 2)
                    if later(i, 1):
                        act.wait_ge(s_h[1], i + 1)
                    nc.scalar.activation(xtT[nxt][:, :, :].rearrange("p k t -> p (k t)"), ps_x1[:, 0:HID], ACT.Copy
                                         ).then_inc(s_tT, 1)
                if y:
                    act.wait_ge(s_yr, i)
                    act.dma_start(y_sorted[bass.ds(r_y, P), :], y_rows[nxt][:, :]).then_inc(s_yst[nxt], 16)
                if h:
                    act.wait_ge(s_ht, i + 1)
                    if later(i, 2):
                        act.wait_ge(s_yd, i - 1)
                    nc.scalar.activation(hidT[par][:, 0:4, :].rearrange("p k t -> p (k t)"), ps_s[:, :], ACT.Copy
                                         ).then_inc(s_hT[0], 1)

            expert_steps(act, expert_stage)

        @block.gpsimd
        def _(pool):
            nc.gpsimd.iota(dist[:, :], pattern=[[1, P]], base=0, channel_multiplier=-1,
                           allow_small_or_imprecise_dtypes=True).then_inc(s_dist, 1)
            nc.gpsimd.memset(visible[:, :], 1.0).then_inc(s_vis, 1)
            pool.wait_ge(s_vis, 1)
            nc.gpsimd.affine_select(out=visible[:, :], in_=visible[:, :], compare_op=ALU.is_ge, fill=0.0,
                                    base=0, pattern=[[1, P]], channel_multiplier=-1).then_inc(s_vis, 1)
            pool.wait_ge(s_vis, 2)
            nc.gpsimd.memset(visible[0:SEQ, SEQ:P], 0.0).then_inc(s_vis, 1)
            pool.wait_ge(s_dist, 1)
            pool.wait_ge(s_vis, 3)
            nc.gpsimd.tensor_tensor(dist[:, :], dist[:, :], visible[:, :], ALU.mult).then_inc(s_dist, 1)
            nc.gpsimd.memset(sq_acc[:, :], 0.0).then_inc(s_zero, 1)
            nc.gpsimd.memset(acc[:, :, :], 0.0).then_inc(s_zero, 1)
            nc.gpsimd.memset(k_all[:, :, :, :], 0.0).then_inc(s_kz, 1)
            nc.gpsimd.memset(v_all[:, :, :, :], 0.0).then_inc(s_vz, 1)
            pool.wait_ge(s_exp, 1)
            nc.gpsimd.tensor_tensor(decay[:, :, :], decay[:, :, :],
                                    visible[:, None, :].to_broadcast([P, H, P]), ALU.mult).then_inc(s_decay, 1)
            nc.gpsimd.memset(zero[:, :], 0.0).then_inc(s_zt, 1)
            nc.gpsimd.iota(numbers[:, :], pattern=[[1, TABLE]], base=0, channel_multiplier=0,
                           allow_small_or_imprecise_dtypes=True).then_inc(s_rc, 1)
            nc.gpsimd.iota(base[:, :], pattern=[[T, E]], base=0, channel_multiplier=0,
                           allow_small_or_imprecise_dtypes=True).then_inc(s_rc, 1)
            nc.gpsimd.memset(sofar[:, 0, :], 0.0).then_inc(s_rc, 1)
            nc.gpsimd.memset(ident[:, :], 0.0).then_inc(s_cm, 1)
            nc.gpsimd.memset(ones[:, :], 1.0).then_inc(s_cm, 1)
            nc.gpsimd.memset(mhalf[:, :], -0.5).then_inc(s_const, 1)
            nc.gpsimd.memset(eps_ln[:, :], EPS_LN).then_inc(s_const, 1)
            pool.wait_ge(s_cm, 2)
            nc.gpsimd.affine_select(out=ident[:, :], in_=ident[:, :], compare_op=ALU.not_equal, fill=1.0,
                                    base=0, pattern=[[-1, P]], channel_multiplier=1).then_inc(s_const, 1)
            nc.gpsimd.affine_select(out=before[:, :], in_=ones[:, :], compare_op=ALU.is_gt, fill=0.0,
                                    base=0, pattern=[[1, P]], channel_multiplier=-1).then_inc(s_const, 1)
            pool.wait_ge(s_zero, 1)

            def add_squares(n, s):
                c = s % 2
                half = sq_acc[:, c * HALF:(c + 1) * HALF]
                pool.wait_ge(s_sq, n + 1)
                if not isinstance(n, int) or n >= 2:
                    pool.wait_ge(s_sqa, n - 1)
                nc.gpsimd.tensor_tensor(half, half, o_sq[s % 2][:, :], ALU.add).then_inc(s_sqa, 1)

            for s in range(4):
                add_squares(s, s)
            with pool.Fori(1, PAIRS) as it:
                for s in range(4):
                    add_squares(4 * it + s, s)
            def inv_root(out, var, eps_ready, done, count, eps):
                if eps is not None:
                    nc.gpsimd.tensor_tensor(var, var, eps, ALU.add).then_inc(eps_ready, 1)
                    pool.wait_ge(eps_ready, count)
                nc.gpsimd.tensor_tensor(out, var, mhalf[:, 0:out.shape[1]], ALU.pow).then_inc(done, 1)

            pool.wait_ge(s_const, 4)
            pool.wait_ge(s_ms, 1)
            for ts in (slice(0, 1), slice(1, TT)):
                inv_root(rms_r[:, ts], ms[:, ts], None, s_rms, 1, None)
            pool.wait_ge(s_wl, 48)

            def scatter(q):
                pool.wait_ge(s_pos, q + 1)
                nc.gpsimd.tensor_tensor(pos_of[:, q, :, :], pick[:, q, :, :],
                                        pos[:, q, None, :].to_broadcast([P, 2, E]), ALU.mult
                                        ).then_inc(s_po2, 1)
                for n, half in enumerate((4, 2, 1)):
                    pool.wait_ge(s_po2, 4 * q + n + 1)
                    nc.gpsimd.tensor_tensor(pos_of[:, q, :, 0:half], pos_of[:, q, :, 0:half],
                                            pos_of[:, q, :, half:2 * half], ALU.add).then_inc(s_po2, 1)
                pool.wait_ge(s_po2, 4 * q + 4)
                nc.gpsimd.tensor_copy(slot_of[:, q, :], pos_of[:, q, :, 0]).then_inc(s_slots, 1)
                pool.wait_ge(s_slots, q + 1)
                if q == 0:
                    pool.wait_ge(s_xz, 32)
                for k in range(2):
                    pool.indirect_dma_start(
                        out=x_sorted, out_offset=bass.IndirectOffsetOnAxis(ap=slot_of[:, q, k:k + 1], axis=0),
                        in_=x2[:, q, :], in_offset=None).then_inc(s_scat, 16)

            for p in CROSS_STEPS:
                if has(p + 3):
                    q = p + 3
                    pool.wait_ge(s_x1, q + 1)
                    nc.gpsimd.tensor_tensor(acc[:, q, :], x_rows[:, q, :], bc[:, :], ALU.add).then_inc(s_x1b, 1)
                if p == TT - 1:
                    scatter(p - 2)
                if has(p + 4):
                    q = p + 4
                    pool.wait_ge(s_m1, q + 1)
                    inv_root(rs1[:, q:q + 1], mv1[:, q, 1:2], s_e1, s_r1, q + 1, eps_ln[:, :])
                if has(p):
                    pool.wait_ge(s_m2, p + 1)
                    inv_root(rs2[:, p:p + 1], mv2[:, p, 1:2], s_e2, s_r2, p + 1, eps_ln[:, :])
                if has(p - 2) and p != TT - 1:
                    scatter(p - 2)

            def gather(k, t):
                pool.indirect_dma_start(out=y_got[k][:, t, :], out_offset=None, in_=y_sorted,
                                        in_offset=bass.IndirectOffsetOnAxis(ap=slot[k][:, t:t + 1], axis=0)
                                        ).then_inc(s_ga[k][t], 16)

            def stored(counts, nth):
                n = [pool.value_load(counts[0:1, par:par + 1], min_val=0, max_val=16 * MAX_TILES)
                     for par in range(2)]
                for par in range(2):
                    pool.wait_ge(s_yst[par], n[par])
                nc.gpsimd.tensor_tensor(seen[:, nth - 1:nth], ones[:, 0:1], ones[:, 0:1], ALU.add).then_inc(s_seen, 1)
                pool.wait_ge(s_seen, nth)

            pool.wait_ge(s_tab, 1)
            nc.gpsimd.tensor_tensor(seen[:, 0:1], ones[:, 0:1], ones[:, 0:1], ALU.add).then_inc(s_seen, 1)
            pool.wait_ge(s_ordered, 1)
            stored(stores_lo, 2)
            for t in range(TT):
                gather(0, t)
            stored(stores_all, 3)
            for t in range(TT):
                gather(1, t)
            for half in range(2):
                ts = slice(half * TT // 2, (half + 1) * TT // 2)
                pool.wait_ge(s_c4, (half + 1) * TT // 2)
                inv_root(rs3[:, ts], mv3[:, ts, 1], s_e3, s_r3, half + 1, eps_ln[:, :].to_broadcast([P, TT // 2]))

        @block.vector
        def _(dve):
            hi = [0]

            dve.wait_ge(s_slope, 16)
            nc.vector.tensor_scalar(slope[:, :], slope[:, :], -1.0, None, ALU.mult).then_inc(s_arg_pre, 1)
            dve.wait_ge(s_arg_pre, 1)
            dve.wait_ge(s_dist, 2)
            nc.vector.tensor_tensor(decay[:, :, :], dist[:, None, :].to_broadcast([P, H, P]),
                                    slope[:, :, None].to_broadcast([P, H, P]), ALU.mult).then_inc(s_arg, 1)

            def split_x(c, base):
                toks = slice(c * HALF, (c + 1) * HALF)
                dve.wait_ge(s_x[c], 16)
                nc.vector.tensor_copy(xh[:, :, toks], x_raw[:, :, toks]).then_inc(s_hi, 1)
                dve.wait_ge(s_hi, base)
                nc.vector.tensor_tensor(xl[:, :, toks], x_raw[:, :, toks], xh[:, :, toks],
                                        ALU.subtract).then_inc(s_xs[c], 1)

            def split_a(i, a, base):
                dve.wait_ge(s_wa[a], 16 * i + 16)
                nc.vector.tensor_copy(wa_h[a][:, :, :, :], wa_raw[a][:, :, :, :]).then_inc(s_hi, 1)
                dve.wait_ge(s_hi, base)
                nc.vector.tensor_tensor(wa_l[a][:, :, :, :], wa_raw[a][:, :, :, :], wa_h[a][:, :, :, :],
                                        ALU.subtract).then_inc(s_wasp[a], 1)

            def split_v(i, base):
                raw = wv_raw[:, :, :, :].rearrange("p k a e -> p k (a e)")
                dve.wait_ge(s_wv, 16 * i + 16)
                nc.vector.tensor_copy(wv_h[:, :, :], raw).then_inc(s_hi, 1)
                dve.wait_ge(s_hi, base)
                nc.vector.tensor_tensor(wv_l[:, :, :], raw, wv_h[:, :, :], ALU.subtract).then_inc(s_wvsp, 1)

            split_x(0, 1)
            split_a(0, 0, 2)
            split_v(0, 3)
            split_x(1, 4)
            dve.wait_ge(s_small, 16)

            def mask(m, s, it_of, early):
                dve.wait_ge(s_s, m + 1)
                if isinstance(m, int) and m == 0:
                    dve.wait_ge(s_decay, 1)
                if not early:
                    dve.wait_ge(s_o, m - 1)
                a = s // 2
                head = decay[:, bass.ds(2 * it_of + a, 1), :] if not isinstance(it_of, int) \
                    else decay[:, 2 * it_of + a:2 * it_of + a + 1, :]
                nc.vector.tensor_tensor(pT[s % 2][:, :].rearrange("p (j i) -> p j i", j=TH),
                                        ps_s[:, :].rearrange("p (j i) -> p j i", j=TH),
                                        head.to_broadcast([P, TH, P]), ALU.mult).then_inc(s_p, 1)

            def gate(m, s):
                dve.wait_ge(s_o, m + 1)
                dve.wait_ge(s_g, m + 1)
                nc.vector.scalar_tensor_tensor(out=go[s % 2][:, :], in0=tg[s % 2][:, :],
                                               scalar=1.0, in1=ps_o[:, :], op0=ALU.add, op1=ALU.mult
                                               ).then_inc(s_go, 1)

            def low(m, s):
                a, c = s // 2, s % 2
                toks = slice(c * HALF, (c + 1) * HALF)
                dve.wait_ge(s_gh, m + 1)
                nc.vector.tensor_tensor(go_l[a][:, toks], go[s % 2][:, :], go_h[a][:, toks],
                                        ALU.subtract).then_inc(s_gl, 1)

            def add_out(i, c):
                for b in range(2):
                    dve.wait_ge(s_y[b], 2 * i + c + 1)
                    part = acc[:, TH * c + 2 * b:TH * c + 2 * b + 2, :].rearrange("p t n -> p (t n)")
                    nc.vector.tensor_tensor(part, part, ps_y[b][:, :], ALU.add).then_inc(s_ya[b], 1)

            def step(it, s, first):
                n = 4 * it + s
                last_it = it - 1 if s == 0 else it
                if not (first and s == 0):
                    mask(n - 1, (s - 1) % 4, last_it, first and s < 3)
                    if not (first and s == 1):
                        low(n - 2, (s - 2) % 4)
                if s == 0:
                    if not first:
                        dve.wait_ge(s_pg, n)
                    split_a(it, 1, 3 * it + 5)
                if not (first and s == 0):
                    if not first and s in (1, 2):
                        dve.wait_ge(s_y[1], 2 * it - 1 + s - 1)
                    gate(n - 1, (s - 1) % 4)
                if s < 2 and not first:
                    add_out(it - 1, s)

            def scale_out(it):
                dve.wait_ge(s_wo, 16 * it + 16)
                for a in range(2):
                    r = rms_w[:, 2 * it + a:2 * it + a + 1] if isinstance(it, int) \
                        else rms_w[:, bass.ds(2 * it + a, 1)]
                    ins = nc.vector.tensor_scalar(wo_s[:, a, :], wo_raw[:, a, :], r, 0.5, ALU.mult, ALU.mult)
                ins.then_inc(s_wos, 1)
                dve.wait_ge(s_wos, it + 1)
                nc.vector.tensor_copy(wo_h[:, :, :], wo_s[:, :, :]).then_inc(s_woh, 1)
                dve.wait_ge(s_woh, it + 1)
                nc.vector.tensor_tensor(wo_l[:, :, :], wo_s[:, :, :], wo_h[:, :, :], ALU.subtract).then_inc(s_wosp, 1)

            def pair(it, first, last):
                for s in range(4):
                    step(it, s, first)
                    if s == 0 and first:
                        dve.wait_ge(s_zero, 2)
                    if s == 2:
                        if not last:
                            dve.wait_ge(s_pg, 4 * it + 2)
                            split_a(it + 1, 0, 3 * it + 6)
                        scale_out(it)
                    if s == 3 and not last:
                        dve.wait_ge(s_pv, 4 * it + 4)
                        split_v(it + 1, 3 * it + 7)

            pair(0, True, False)
            with dve.Fori(1, PAIRS - 1) as it:
                pair(it, False, False)
            pair(PAIRS - 1, False, True)
            mask(STEPS - 1, 3, PAIRS - 1, False)
            low(STEPS - 2, 2)
            gate(STEPS - 1, 3)
            low(STEPS - 1, 3)
            add_out(PAIRS - 1, 0)

            dve.wait_ge(s_pms, 1)
            nc.vector.tensor_scalar(ms[:, :], ps_q[:, 0:TT], 1.0 / (H * D), EPS_RMS, ALU.mult, ALU.add
                                    ).then_inc(s_ms, 1)
            add_out(PAIRS - 1, 1)
            dve.wait_ge(s_xr, 16)
            dve.wait_ge(s_va, 2)
            dve.wait_ge(s_kl, 16 * 16)
            dve.wait_ge(s_rms, 1)
            for b in range(2):
                dve.wait_ge(s_ya[b], 2 * PAIRS)

            tt, tred = nc.vector.tensor_tensor, nc.vector.tensor_reduce
            for p in CROSS_STEPS:
                if has(p + 3):
                    q = p + 3
                    dve.wait_ge(s_r1, q + 1)
                    nc.vector.tensor_scalar(x_rows[:, q, :], acc[:, q, :], mv1[:, q, 0:1], rs1[:, q:q + 1],
                                            ALU.subtract, ALU.mult).then_inc(s_x1, 1)
                if has(p + 2):
                    q = p + 2
                    dve.wait_ge(s_sc, q + 1)
                    tred(pmax[:, :].rearrange("p (r c) -> p r c", r=NR),
                         sc_all[:, :, 0:2 * P].rearrange("p r (c t) -> p r c t", t=SEQ), AX_X, ALU.max
                         ).then_inc(s_mx, 1)
                if has(p - 1):
                    q = p - 1
                    dve.wait_ge(s_r2, q + 1)
                    nc.vector.tensor_scalar(x2[:, q, :], z2[q % 2][:, :], mv2[:, q, 0:1], rs2[:, q:q + 1],
                                            ALU.subtract, ALU.mult).then_inc(s_x2, 1)
                if has(p):
                    dve.wait_ge(s_pe, p + 1)
                    nc.vector.reciprocal(prec[:, :], prob_sum[p % 2][:, :]).then_inc(s_pr, 1)
                if has(p):
                    dve.wait_ge(s_pvx, p + 1)
                    dve.wait_ge(s_pr, p + 1)
                    if p >= 1:
                        dve.wait_ge(s_xot, p)
                    for b in range(2):
                        rows = slice(b * SEQ, (b + 1) * SEQ)
                        src = ps_x[:, :].rearrange("p (j b h d) -> p j b h d", b=2, h=2, d=HD)[rows, :, b, :, :]
                        tt(xo[rows, :].rearrange("p (j h d) -> p j h d", h=2, d=HD), src,
                           prec[rows, :].rearrange("p (j h) -> p j h", h=2)[:, :, :, None]
                           .to_broadcast([SEQ, XH // 2, 2, HD]), ALU.mult).then_inc(s_xo, 1)
                if has(p - 2):
                    q = p - 2
                    dve.wait_ge(s_cnt, q + 1)
                    tt(pos[:, q, :], ps_x1[:, E:2 * E], base[:, :], ALU.add).then_inc(s_pos, 1)
                if has(p + 2):
                    q = p + 2
                    dve.wait_ge(s_mx, q + 1)
                    if q >= 2:
                        dve.wait_ge(s_pt[1], q - 1)
                    for f in range(2):
                        tt(prob[q % 2][:, 8 * f:8 * f + 8, :].rearrange("p (r h) t -> p r h t", r=NR),
                           sc_all[:, :, f * P:(f + 1) * P].rearrange("p r (h t) -> p r h t", h=2),
                           pmax[:, :].rearrange("p (r f h) -> p r f h", r=NR, f=2)[:, :, f, :, None]
                           .to_broadcast([P, NR, 2, SEQ]), ALU.subtract).then_inc(s_sub, 1)
                if has(p + 4):
                    q = p + 4
                    if q == 1:
                        dve.wait_ge(s_rms, 2)
                    nc.vector.scalar_tensor_tensor(out=acc[:, q, :], in0=acc[:, q, :], scalar=rms_r[:, q:q + 1],
                                                   in1=x_rows[:, q, :], op0=ALU.mult, op1=ALU.add).then_inc(s_z1, 1)
                    dve.wait_ge(s_z1, q + 1)
                    nc.vector.bn_stats(st1[:, q, :], acc[:, q, :]).then_inc(s_b1, 1)
                    dve.wait_ge(s_b1, q + 1)
                    nc.vector.bn_aggr(mv1[:, q, :], st1[:, q, :]).then_inc(s_m1, 1)
                if has(p):
                    dve.wait_ge(s_wcd, p + 1)
                    dve.wait_ge(s_x1b, p + 1)
                    tt(z2[p % 2][:, :], ps_x[:, 0:HID], acc[:, p, :], ALU.add).then_inc(s_z2, 1)
                    dve.wait_ge(s_z2, p + 1)
                    nc.vector.bn_stats(st2[:, p, :], z2[p % 2][:, :]).then_inc(s_b2, 1)
                    dve.wait_ge(s_b2, p + 1)
                    nc.vector.bn_aggr(mv2[:, p, :], st2[:, p, :]).then_inc(s_m2, 1)
                if has(p - 1):
                    q = p - 1
                    dve.wait_ge(s_rt, q + 1)
                    nc.vector.tensor_copy(logit[:, q, :], ps_x1[:, 0:E]).then_inc(s_lg, 1)
                    dve.wait_ge(s_lg, q + 1)
                    nc.vector.max(best[:, q, :], logit[:, q, :]).then_inc(s_sort, 1)
                    dve.wait_ge(s_sort, q + 1)
                    nc.vector.max_index(best_at[:, q, :], best[:, q, :], logit[:, q, :]).then_inc(s_at, 1)
                    dve.wait_ge(s_at, q + 1)
                    nc.vector.tensor_copy(chosen[:, q, :], best_at[:, q, 0:2]).then_inc(s_ch, 1)
                    dve.wait_ge(s_ch, q + 1)
                    tt(pick[:, q, :, :], numbers[:, None, 0:E].to_broadcast([P, 2, E]),
                       chosen[:, q, :, None].to_broadcast([P, 2, E]), ALU.is_equal).then_inc(s_pk2, 1)
                    dve.wait_ge(s_pk2, q + 1)
                    tt(both[:, q, :], pick[:, q, 0, :], pick[:, q, 1, :], ALU.add).then_inc(s_both, 1)
                    dve.wait_ge(s_both, 2 * q + 1)
                    tt(sofar[:, q + 1, :], sofar[:, q, :], both[:, q, :], ALU.add).then_inc(s_both, 1)

            made = [0]

            def table_step(ins):
                made[0] += 1
                ins.then_inc(s_r, 1)
                dve.wait_ge(s_r, made[0])

            ts1 = nc.vector.tensor_scalar
            NT = TABLE
            dve.wait_ge(s_tot, 1)
            table_step(nc.vector.tensor_copy(counts[:, :], ps_s[:, 0:E]))
            table_step(ts1(counts[:, :], counts[:, :], 1.0 / P, None, ALU.mult))
            table_step(tt(more[:, :, :], counts[:, :, None].to_broadcast([P, E, TT]),
                          numbers[:, None, 0:TT].to_broadcast([P, E, TT]), ALU.is_gt))
            table_step(tred(tiles_of[:, :], more[:, :, :], AX_X, ALU.add))
            src = tiles_of
            for i, hop in enumerate((1, 2, 4)):
                dst = run[i % 2]
                nc.vector.tensor_copy(dst[:, 0:hop], src[:, 0:hop])
                table_step(tt(dst[:, hop:], src[:, hop:], src[:, 0:E - hop], ALU.add))
                src = dst
            end = src
            table_step(tt(past[:, :, :], end[:, None, 0:E - 1].to_broadcast([P, NT, E - 1]),
                          numbers[:, :, None].to_broadcast([P, NT, E - 1]), ALU.is_le))
            table_step(ts1(skip[:, :], tiles_of[:, 0:E - 1], -float(P), float(T), ALU.mult, ALU.add))
            table_step(tt(skips[:, :, :], past[:, :, :], skip[:, None, :].to_broadcast([P, NT, E - 1]), ALU.mult))
            table_step(tred(row_f[:, :], skips[:, :, :], AX_X, ALU.add))
            table_step(nc.vector.scalar_tensor_tensor(out=row_f[:, :], in0=numbers[:, :], scalar=float(P),
                                                      in1=row_f[:, :], op0=ALU.mult, op1=ALU.add))
            ts1(row[:, :], row_f[:, :], float(E * T - P), None, ALU.min)
            table_step(ts1(halves_of[:, 0, :], numbers[:, 0:MIN_TILES], 2.0, end[:, E - 1:E], ALU.mult, ALU.is_lt))
            table_step(tred(pairs_f[:, 0:1], halves_of[:, 0, :], AX_X, ALU.add))
            ts1(steps[:, 0:1], pairs_f[:, 0:1], 2.0, -6.0, ALU.mult, ALU.add)
            table_step(nc.vector.scalar_tensor_tensor(out=parity_f[:, :], in0=pairs_f[:, 0:1], scalar=-2.0,
                                                      in1=end[:, E - 1:E], op0=ALU.mult, op1=ALU.add))
            ts1(steps[:, 1:2], parity_f[:, :], 1.0, None, ALU.add).then_inc(s_row, 1)
            table_step(tred(expert[:, :], past[:, :, :], AX_X, ALU.add))
            table_step(ts1(wrap[:, :], expert[:, :], float(SLOTS), -float(SLOTS), ALU.is_ge, ALU.mult))
            tt(place[:, :], expert[:, :], wrap[:, :], ALU.add)
            ts1(need[:, :], expert[:, :], 16.0, 16.0, ALU.mult, ALU.add)
            nc.vector.tensor_copy(which[:, :], expert[:, :])
            table_step(ts1(halves_of[:, 1, :], numbers[:, 0:MIN_TILES], 2.0, end[:, E - 2:E - 1],
                           ALU.mult, ALU.is_lt))
            table_step(tred(pairs_f[:, 1:2], halves_of[:, 1, :], AX_X, ALU.add))
            ts1(stores_lo[:, 0:1], pairs_f[:, 1:2], 16.0, None, ALU.mult)
            tt(w_part[:, 0, 0:1], end[:, E - 2:E - 1], pairs_f[:, 1:2], ALU.subtract)
            table_step(tt(w_part[:, 1, 0:1], end[:, E - 1:E], pairs_f[:, 0:1], ALU.subtract))
            ts1(stores_lo[:, 1:2], w_part[:, 0, 0:1], 16.0, None, ALU.mult)
            ts1(stores_all[:, 0:1], pairs_f[:, 0:1], 16.0, None, ALU.mult)
            ts1(stores_all[:, 1:2], w_part[:, 1, 0:1], 16.0, None, ALU.mult)
            ts1(free_at[:, :], end[:, :], 1.0, None, ALU.add).then_inc(s_tab, 1)

            dve.wait_ge(s_po2, 4 * TT)
            tt(slot[0][:, :], pos_of[:, :, 0, 0], pos_of[:, :, 1, 0], ALU.min)
            tt(slot[1][:, :], pos_of[:, :, 0, 0], pos_of[:, :, 1, 0], ALU.max).then_inc(s_ordered, 1)

            steps_w = [0]

            def weight_step(ins):
                steps_w[0] += 1
                ins.then_inc(s_w, 1)
                dve.wait_ge(s_w, steps_w[0])

            tt(ratio[:, :], best[:, :, 1], best[:, :, 0], ALU.subtract).then_inc(s_dif, 1)
            tt(lower[:, :], chosen[:, :, 0], chosen[:, :, 1], ALU.is_lt)
            tt(upper[:, :], chosen[:, :, 0], chosen[:, :, 1], ALU.is_gt)
            dve.wait_ge(s_rexp, 1)
            weight_step(ts1(w_best[0][:, :], ratio[:, :], 1.0, None, ALU.add))
            weight_step(nc.vector.reciprocal(w_best[0][:, :], w_best[0][:, :]))
            weight_step(tt(w_best[1][:, :], w_best[0][:, :], ratio[:, :], ALU.mult))
            tt(w_part[:, 0, :], w_best[0][:, :], lower[:, :], ALU.mult)
            tt(w_part[:, 1, :], w_best[1][:, :], upper[:, :], ALU.mult)
            tt(w_part[:, 2, :], w_best[0][:, :], upper[:, :], ALU.mult)
            weight_step(tt(w_part[:, 3, :], w_best[1][:, :], lower[:, :], ALU.mult))
            tt(weight[0][:, :], w_part[:, 0, :], w_part[:, 1, :], ALU.add)
            weight_step(tt(weight[1][:, :], w_part[:, 2, :], w_part[:, 3, :], ALU.add))

            nc.vector.memset(counts[:, :], 0.0).then_inc(s_h[1], 1)

            def expert_stage(i, par, h, t, y):
                if h:
                    for c in range(2):
                        dve.wait_ge(s_si[c], i + 1)
                        if later(i, 1):
                            dve.wait_ge(s_ht, i)
                        tt(hid[:, c * HB:(c + 1) * HB], act_h[:, c * HB:(c + 1) * HB],
                           sc_all[:, 2 * c + 1, 0:HB], ALU.mult).then_inc(s_hm[c], 1)
                if y:
                    dve.wait_ge(s_yd, i)
                    if later(i, 3):
                        dve.wait_ge(s_yst[1 - par], 8 * (i - 1) if par else 8 * (i - 2))
                    nc.vector.tensor_copy(y_rows[1 - par][:, :], ps_x[:, 0:HID]).then_inc(s_yr, 1)
                if h:
                    dve.wait_ge(s_ht, i + 1)
                    if later(i, 2):
                        dve.wait_ge(s_yd, i - 1)
                    nc.vector.tensor_copy(hidT[par][:, 4, :], ps_o[:, 0:P])
                    nc.vector.tensor_copy(hidT[par][0:ITAIL, 5, :], ps_o[0:ITAIL, P:2 * P]).then_inc(s_hT[1], 1)

            expert_steps(dve, expert_stage)

            for t in range(TT):
                dve.wait_ge(s_ga[0][t], 16)
                nc.vector.scalar_tensor_tensor(out=acc[:, t, :], in0=y_got[0][:, t, :], scalar=weight[0][:, t:t + 1],
                                               in1=x2[:, t, :], op0=ALU.mult, op1=ALU.add).then_inc(s_c1, 1)
            for t in range(TT):
                dve.wait_ge(s_ga[1][t], 16)
                dve.wait_ge(s_c1, t + 1)
                nc.vector.scalar_tensor_tensor(out=acc[:, t, :], in0=y_got[1][:, t, :], scalar=weight[1][:, t:t + 1],
                                               in1=acc[:, t, :], op0=ALU.mult, op1=ALU.add).then_inc(s_c2, 1)
                dve.wait_ge(s_c2, t + 1)
                nc.vector.bn_stats(st3[:, t, :], acc[:, t, :]).then_inc(s_c3, 1)
                dve.wait_ge(s_c3, t + 1)
                nc.vector.bn_aggr(mv3[:, t, :], st3[:, t, :]).then_inc(s_c4, 1)
            for half in range(2):
                dve.wait_ge(s_r3, half + 1)
                for u in range(half * TT // 2, (half + 1) * TT // 2):
                    ts1(acc[:, u, :], acc[:, u, :], mv3[:, u, 0:1], rs3[:, u:u + 1],
                        ALU.subtract, ALU.mult).then_inc(s_x3, 1)

        @block.tensor
        def _(pe):
            mm = nc.tensor.matmul

            def keep_busy(n, out, by, moving):
                for _ in range(n):
                    mm(out, by, moving, start=True, stop=True)

            def project(bank, a, which, c, done):
                toks = slice(c * HALF, (c + 1) * HALF)
                passes = [(w, x, k) for w, x in ((wa_l[a], xh), (wa_h[a], xl), (wa_h[a], xh)) for k in range(KT)]
                for i, (w, x, k) in enumerate(passes):
                    ins = mm(bank[:, :], w[:, k, which, :], x[:, k, toks],
                             start=(i == 0), stop=(i == len(passes) - 1))
                ins.then_inc(done, 1)

            def values(n_v, c, part):
                if not isinstance(n_v, int) or n_v > 0:
                    pe.wait_ge(s_v, n_v)
                passes = [(x, w, k) for x, w in ((xh, wv_l), (xl, wv_h), (xh, wv_h)) for k in range(KT)]
                for j in range(2):
                    t0 = c * HALF + (2 * part + j) * P
                    for i, (x, w, k) in enumerate(passes):
                        ins = mm(ps_v[:, 2 * j * D:2 * (j + 1) * D], x[:, k, t0:t0 + P], w[:, k, :],
                                 start=(i == 0), stop=(i == len(passes) - 1))
                ins.then_inc(s_pv, 1)

            def scores(m, par):
                pe.wait_ge(s_q, m + 1)
                pe.wait_ge(s_k, m + 1)
                if not isinstance(m, int) or m > 0:
                    pe.wait_ge(s_p, m)
                for j in range(TH):
                    t = slice(j * P, (j + 1) * P)
                    ins = mm(ps_s[:, t], kT[par][:, t], qT[par][:, t], start=True, stop=True)
                ins.then_inc(s_s, 1)

            def attend(m, s, it_of):
                a, c = s // 2, s % 2
                pe.wait_ge(s_p, m + 1)
                pe.wait_ge(s_v, 4 * it_of + 2 * c + 2)
                if not isinstance(m, int) or m > 0:
                    pe.wait_ge(s_sq, m)
                for j in range(TH):
                    t = slice(j * P, (j + 1) * P)
                    ins = mm(ps_o[:, t], v_sb[c][:, j, a, :], pT[s % 2][:, t], start=True, stop=True)
                ins.then_inc(s_o, 1)

            def out_product(i, c):
                pe.wait_ge(s_gl, 4 * i + 3 + c)
                pe.wait_ge(s_wosp, i + 1)
                for b in range(2):
                    if not (isinstance(i, int) and i == 0 and c == 0):
                        pe.wait_ge(s_ya[b], 2 * i + c)
                    for t in range(2):
                        t0 = (TH * c + 2 * b + t) * P
                        passes = [(g[a], w, a) for g, w in ((go_l, wo_h), (go_h, wo_l), (go_h, wo_h))
                                  for a in range(2)]
                        for n, (g, w, a) in enumerate(passes):
                            ins = mm(ps_y[b][:, t * HID:(t + 1) * HID], g[:, t0:t0 + P], w[:, a, :],
                                     start=(n == 0), stop=(n == len(passes) - 1))
                    ins.then_inc(s_y[b], 1)

            def step(it, s, first):
                n = 4 * it + s
                a, c = s // 2, s % 2
                lag, lag_s, lag_it = n - 1, (s - 1) % 4, (it - 1 if s == 0 else it)
                started = not (first and s == 0)
                if c == 0:
                    pe.wait_ge(s_wasp[a], it + 1)
                if started:
                    pe.wait_ge(s_q, n)
                project(ps_q, a, 0, c, s_pq)
                if s == 0:
                    pe.wait_ge(s_wvsp, it + 1)
                if s < 2:
                    values(4 * it + 2 * s, c, 0)
                if started:
                    scores(lag, 1 - s % 2)
                    pe.wait_ge(s_k, n)
                project(ps_k, a, 1, c, s_pk)
                if s < 2:
                    values(4 * it + 2 * s + 1, c, 1)
                if started:
                    attend(lag, lag_s, lag_it)
                    pe.wait_ge(s_g, n)
                project(ps_g, a, 2, c, s_pg)
                if s < 2 and not first:
                    out_product(it - 1, s)

            pe.wait_ge(s_vis, 3)
            keep_busy(18, ps_s[:, 0:P], visible[:, :], visible[:, :])
            for s in range(4):
                if s < 2:
                    pe.wait_ge(s_xs[s], 1)
                step(0, s, True)
            with pe.Fori(1, PAIRS) as it:
                for s in range(4):
                    step(it, s, False)
            scores(STEPS - 1, 1)
            out_product(PAIRS - 1, 0)
            attend(STEPS - 1, 3, PAIRS - 1)
            pe.wait_ge(s_wl, 48)
            pe.wait_ge(s_const, 4)
            keep_busy(6, ps_q[:, 0:HID], ones[:, :], wc[:, 0, :])
            pe.wait_ge(s_sqa, STEPS)
            for t in range(TT):
                ins = mm(ps_q[:, t:t + 1], sq_acc[:, t * P:(t + 1) * P], ones[:, 0:1], start=True, stop=True)
            ins.then_inc(s_pms, 1)
            out_product(PAIRS - 1, 1)

            pe.wait_ge(s_sq, STEPS)
            pe.wait_ge(s_ya[0], 2 * PAIRS)
            keep_busy(4, ps_s[:, 0:HID], ones[:, :], wc[:, 0, :])

            def turn(bank, src, done, n=KT):
                for k in range(n):
                    ins = nc.tensor.transpose(bank[:, k * P:(k + 1) * P], src(k), ident[:, :])
                ins.then_inc(done, 1)

            for p in CROSS_STEPS:
                if has(p):
                    pe.wait_ge(s_pe, p + 1)
                    if p >= 1:
                        if p >= 2:
                            pe.wait_ge(s_x2T, p - 1)
                        pe.wait_ge(s_x1T, min(p + 3, TT))
                    elif p == 0:
                        pe.wait_ge(s_x1T, 3)
                    for b in range(2):
                        if p >= 1:
                            pe.wait_ge(s_pT[b], p)
                        turn(ps_pt[b], lambda j: prob[p % 2][:, 8 * b + 2 * j:8 * b + 2 * j + 2, :]
                             .rearrange("p h t -> p (h t)"), s_pt[b], 4)
                if has(p + 2):
                    q = p + 2
                    pe.wait_ge(s_x1T, q + 1)
                    if q == 0:
                        pe.wait_ge(s_ms, 1)
                    else:
                        pe.wait_ge(s_sub, 2 * q)
                    for f in range(2):
                        for b in range(2):
                            for r in range(NR):
                                rows = slice(r * ROWS, (r + 1) * ROWS)
                                cols = slice(b * SEQ, (b + 1) * SEQ)
                                ins = mm(ps_sc[r][cols, f * P:(f + 1) * P], x1T[q % 2][rows, f, cols],
                                         k_all[rows, 2 * q + b, f, :], start=True, stop=True)
                    ins.then_inc(s_sc, 1)
                if has(p):
                    if p >= 1:
                        pe.wait_ge(s_z2, p)
                    keep_busy(1, ps_x[:, 0:HID], ones[:, :], wc[:, 0, :])
                if has(p + 3):
                    q = p + 3
                    pe.wait_ge(s_x1, q + 1)
                    if has(p):
                        pe.wait_ge(s_pT[1], p + 1)
                    elif q >= 1:
                        pe.wait_ge(s_x1T, q)
                    turn(ps_o, lambda k: x_rows[:, q, k * P:(k + 1) * P], s_x1t)
                if has(p):
                    for b in range(2):
                        pe.wait_ge(s_pT[b], p + 1)
                    for j in range(XH // 2):
                        f, r = j // NR, j % NR
                        ins = mm(ps_x[:, 64 * j:64 * j + 64], probT[f][:, r, :],
                                 v_all[:, 2 * p:2 * p + 2, 2 * f + r // 2, :], start=True, stop=True)
                    ins.then_inc(s_pvx, 1)
                if has(p - 1):
                    q = p - 1
                    pe.wait_ge(s_x2, q + 1)
                    if has(p):
                        pe.wait_ge(s_pT[0], p + 1)
                    else:
                        pe.wait_ge(s_x2T, q)
                    turn(ps_s, lambda k: x2[:, q, k * P:(k + 1) * P], s_x2t)
                if has(p - 2):
                    q = p - 2
                    pe.wait_ge(s_both, 2 * q + 2)
                    pe.wait_ge(s_lg, q + 1)
                    if q == TT - 1:
                        pe.wait_ge(s_x2T, TT)
                        mm(ps_s[:, 0:E], ones[:, :], sofar[:, TT, :], start=True, stop=True).then_inc(s_tot, 1)
                    mm(ps_x1[:, E:2 * E], ones[:, :], sofar[:, q, :], start=True, stop=False)
                    mm(ps_x1[:, E:2 * E], before[:, :], both[:, q, :], start=False, stop=True).then_inc(s_cnt, 1)
                if has(p):
                    pe.wait_ge(s_x1T, min(p + 4, TT))
                    keep_busy(1, ps_o[:, 0:HID], ones[:, :], wc[:, 0, :])
                if has(p - 1):
                    q = p - 1
                    pe.wait_ge(s_x2T, q + 1)
                    if q >= 1:
                        pe.wait_ge(s_pos, q)
                    for k in range(KT):
                        ins = mm(ps_x1[:, 0:E], x2T[:, k, :], wg[:, k, :], start=(k == 0), stop=(k == KT - 1))
                    ins.then_inc(s_rt, 1)
                if has(p):
                    pe.wait_ge(s_xo, 2 * p + 2)
                    turn(ps_x, lambda k: xo[:, k * P:(k + 1) * P], s_xot)
                if has(p):
                    keep_busy(1, ps_s[:, 0:HID], ones[:, :], wc[:, 0, :])
                elif has(p + 2):
                    keep_busy(3, ps_s[:, 0:HID], ones[:, :], wc[:, 0, :])
                if has(p):
                    pe.wait_ge(s_xoT, p + 1)
                    for k in range(KT):
                        ins = mm(ps_x[:, 0:HID], xoT[:, k, :], wc[:, k, :], start=(k == 0), stop=(k == KT - 1))
                    ins.then_inc(s_wcd, 1)

            keep_busy(14, ps_o[:, 0:HID], ones[:, :], wc[:, 0, :])
            pe.wait_ge(s_tab, 1)

            def weights_of(i):
                return (pe.value_load(one(need, i), min_val=16, max_val=16 * E),
                        pe.value_load(one(place, i), min_val=0, max_val=SLOTS - 1))

            first_weights = weights_of(0)

            def expert_stage(i, par, h, t, y):
                nxt = 1 - par
                if h:
                    loads, at = weights_of(i) if later(i, 1) else first_weights
                    pe.wait_ge(s_tT, i + 1)
                    pe.wait_ge(s_w13, loads)
                    for c in range(2):
                        if later(i, 1):
                            pe.wait_ge(s_hm[c], i)
                        for g in range(2):
                            for k in range(KT):
                                col = g * INTER + c * HB
                                ins = mm(sc_all[:, 2 * c + g, 0:HB], xtT[par][:, k, :],
                                         w13[:, bass.ds(at, 1), k, col:col + HB].rearrange("p a n -> p (a n)"),
                                         start=(k == 0), stop=(k == KT - 1))
                        ins.then_inc(s_h[c], 1)
                if t:
                    pe.wait_ge(s_xt[nxt], 8 * (i + 3) if par else 8 * (i + 2))
                    if later(i, 0):
                        pe.wait_ge(s_tT, i + 1)
                    turn(ps_x1, lambda k: xt_rows[nxt][:, k * P:(k + 1) * P], s_tt)
                if y:
                    at1 = pe.value_load(one(which, i - 1), min_val=0, max_val=E - 1)
                    if not later(i, 2):
                        pe.wait_ge(s_w2, 32 * E)
                    for b in range(2):
                        pe.wait_ge(s_hT[b], i)
                    if later(i, 2):
                        pe.wait_ge(s_yr, i - 1)
                    for k in range(ITILES):
                        rows = P if k < ITILES - 1 else ITAIL
                        ins = mm(ps_x[:, 0:HID], hidT[nxt][0:rows, k, :],
                                 w2[0:rows, bass.ds(at1, 1), k, :].rearrange("p a n -> p (a n)"),
                                 start=(k == 0), stop=(k == ITILES - 1))
                    ins.then_inc(s_yd, 1)
                if h:
                    for c in range(2):
                        pe.wait_ge(s_hm[c], i + 1)
                    if later(i, 1):
                        for b in range(2):
                            pe.wait_ge(s_hT[b], i)
                    for k in range(ITILES):
                        rows = P if k < ITILES - 1 else ITAIL
                        bank, col = (ps_s, k) if k < 4 else (ps_o, k - 4)
                        ins = nc.tensor.transpose(bank[0:rows, col * P:(col + 1) * P], hid[:, k * P:k * P + rows],
                                                  ident[:, :])
                    ins.then_inc(s_ht, 1)

            expert_steps(pe, expert_stage)


def kernel(**inputs):
    import numpy as np
    import concourse.bacc as bacc
    from concourse.bass_utils import run_bass_kernel_spmd

    f = {k: np.ascontiguousarray(v) for k, v in inputs.items()}
    x = f["x"].reshape(T, HID)
    wqkv = f["L0_attn_w_qkv"].reshape(KT, P, 3, H, D)
    wgate = f["L0_attn_w_gate"].reshape(KT, P, 1, H, D)
    wqkg = np.concatenate([wqkv[:, :, 0:2], wgate], axis=2)
    arrays = {
        "xT": x.T,
        "x": x,
        "wa": wqkg.transpose(3, 1, 0, 2, 4),
        "wv": wqkv[:, :, 2].reshape(KT, P, PAIRS, 2, D).transpose(2, 1, 0, 3, 4),
        "wo": f["L0_attn_w_out"].reshape(PAIRS, 2, D, HID).transpose(0, 2, 1, 3),
        "ctx": f["ctx_512"].reshape(T, CTX),
        "ctxT": f["ctx_512"].reshape(T, CTX).T,
        "wcT": f["L0_xattn_Wc"].T,
        "bc": f["L0_xattn_bc"].reshape(1, HID),
        "wgT": f["L0_ffn_Wg"].T,
        "w13": np.stack([f["L0_ffn_w1"], f["L0_ffn_w3"]], 1).reshape(E, 2 * INTER, KT, P).transpose(0, 3, 2, 1),
        "w2a": f["L0_ffn_w2"].transpose(0, 2, 1)[:, :(ITILES - 1) * P].reshape(E, ITILES - 1, P, HID)
        .transpose(0, 2, 1, 3),
        "w2b": f["L0_ffn_w2"].transpose(0, 2, 1)[:, (ITILES - 1) * P:],
        "rms": f["L0_attn_rms_weight"].reshape(H, D).T,
        "slope": f["L0_attn_slope_rate"].reshape(1, H),
    }
    nc = bacc.Bacc("TRN2", target_bir_lowering=False, num_devices=1)
    d, sent = {}, {}
    for name, a in arrays.items():
        a = np.ascontiguousarray(a)
        sent[f"in_{name}"] = a
        d[name] = nc.dram_tensor(f"in_{name}", a.shape, mybir.dt.from_np(a.dtype), kind="ExternalInput").ap()
    d["out"] = nc.dram_tensor("out_x", (T, HID), F32, kind="ExternalOutput").ap()
    decoder_layer(nc, d)
    got = run_bass_kernel_spmd(nc, [sent], core_ids=[0])
    return got.results[0]["out_x"].reshape(BATCHES, SEQ, HID)
```
